# Optimizing a Trainium2 kernel written in Bass

```python
import numpy as np
import jax
import jax.numpy as jnp

def _softmax(x, axis=-1):
    return jax.nn.softmax(x, axis=axis)

def _gelu(x):
    return jax.nn.gelu(x, approximate=True)

def _silu(x):
    return jax.nn.silu(x)

def _sigmoid(x):
    return jax.nn.sigmoid(x)

def _layernorm(x, axis=-1, eps=1e-05):
    m = jnp.mean(x, axis=axis, keepdims=True)
    v = jnp.var(x, axis=axis, keepdims=True)
    return (x - m) / jnp.sqrt(v + eps)

def _scatter_add(tgt, idx, src, axis=0):
    return tgt.at[idx].add(src)

def _segment_sum(src, seg, n):
    return jax.ops.segment_sum(src, seg, n)
kernel_name = 'mk_xattn_seq_d4_seqx_r8_3badca'

def setup_inputs(seed: int=0):
    np.random.seed(seed)
    _w = jnp.asarray

    def _rec_inputs():
        import jax
        import jax.numpy as jnp
        _rk = jax.random.key(seed)
        x = -0.000125 + 0.9999 * jax.random.normal(jax.random.fold_in(_rk, 1), (16, 128, 128), jnp.float32)
        _lenS = 128 - jax.random.randint(jax.random.fold_in(_rk, 7), (16,), 0, max(1, 128 // 4) + 1, jnp.int32)
        _lenS2 = 128 - jax.random.randint(jax.random.fold_in(_rk, 8), (16,), 0, max(1, 128 // 4) + 1, jnp.int32)
        _ctx_2048P = jax.random.normal(jax.random.fold_in(_rk, 11), (16, 16, 256), jnp.float32)
        _ctx_2048c = jax.random.dirichlet(jax.random.fold_in(_rk, 511), 0.3 * jnp.ones((16,), jnp.float32), (16, 128))
        _ctx_2048t = jnp.einsum('bsk,bkd->bsd', _ctx_2048c, _ctx_2048P)
        _ctx_2048t = _ctx_2048t * jax.lax.rsqrt(jnp.mean(jnp.square(_ctx_2048t)) + 1e-12) * 0.953939
        ctx_2048 = 5.36139e-06 + 1.00015 * (_ctx_2048t + 0.3 * jax.random.normal(jax.random.fold_in(_rk, 611), (16, 128, 256), jnp.float32))
        _validS = jnp.arange(128)[None, :] < _lenS[:, None]
        _validS2 = jnp.arange(128)[None, :] < _lenS2[:, None]
        _causal = jnp.tril(jnp.ones((128, 128), dtype=bool))
        mask_S_fk1 = jnp.where(_validS[0], 1.0, 0.0).astype(jnp.float32)
        mask_S_fk0 = jnp.where(_validS[0], 0.0, 1.0).astype(jnp.float32)
        return (x, ctx_2048, mask_S_fk1, mask_S_fk0)
    x, ctx_2048, mask_S_fk1, mask_S_fk0 = _rec_inputs()

    def _L0_xattn_setup():
        import jax, jax.numpy as jnp
        import numpy as np
        HEADS = 16
        HEAD_DIM = 64
        SUPPRESS = 20.0
        key = jax.random.key(seed)
        ks = jax.random.split(key, 8)
        B, HW, C, T, CT = (8, 512, 128, 77, 256)
        inner = HEADS * HEAD_DIM
        scale = 0.02
        return {'hidden_states': jax.random.normal(ks[0], (B, HW, C), jnp.float32), 'encoder_hidden_states': jax.random.normal(ks[1], (B, T, CT), jnp.float32), 'mask_A': (jax.random.uniform(ks[2], (HW,)) > 0.5).astype(jnp.float32), 'mask_B': (jax.random.uniform(ks[3], (HW,)) > 0.5).astype(jnp.float32), 'Wq': jax.random.normal(ks[4], (C, inner), jnp.float32) * scale, 'Wk': jax.random.normal(ks[5], (CT, inner), jnp.float32) * scale, 'Wv': jax.random.normal(ks[6], (CT, inner), jnp.float32) * scale, 'Wo': jax.random.normal(ks[7], (inner, C), jnp.float32) * scale, 'bo': jnp.zeros((C,), jnp.float32), 'token_indices_A': jnp.array([2, 3], dtype=jnp.int64), 'token_indices_B': jnp.array([5, 6], dtype=jnp.int64)}
    _L0_xattn_all = _L0_xattn_setup()
    _L0_xattn_in = {k: v for k, v in _L0_xattn_all.items() if k in ('Wq', 'Wk', 'Wv', 'Wo', 'bo', 'token_indices_A', 'token_indices_B')}
    del _L0_xattn_all

    def _L1_xattn_setup():
        import jax, jax.numpy as jnp
        import numpy as np
        HEADS = 16
        HEAD_DIM = 64
        SUPPRESS = 20.0
        key = jax.random.key(seed)
        ks = jax.random.split(key, 8)
        B, HW, C, T, CT = (8, 512, 128, 77, 256)
        inner = HEADS * HEAD_DIM
        scale = 0.02
        return {'hidden_states': jax.random.normal(ks[0], (B, HW, C), jnp.float32), 'encoder_hidden_states': jax.random.normal(ks[1], (B, T, CT), jnp.float32), 'mask_A': (jax.random.uniform(ks[2], (HW,)) > 0.5).astype(jnp.float32), 'mask_B': (jax.random.uniform(ks[3], (HW,)) > 0.5).astype(jnp.float32), 'Wq': jax.random.normal(ks[4], (C, inner), jnp.float32) * scale, 'Wk': jax.random.normal(ks[5], (CT, inner), jnp.float32) * scale, 'Wv': jax.random.normal(ks[6], (CT, inner), jnp.float32) * scale, 'Wo': jax.random.normal(ks[7], (inner, C), jnp.float32) * scale, 'bo': jnp.zeros((C,), jnp.float32), 'token_indices_A': jnp.array([2, 3], dtype=jnp.int64), 'token_indices_B': jnp.array([5, 6], dtype=jnp.int64)}
    _L1_xattn_all = _L1_xattn_setup()
    _L1_xattn_in = {k: v for k, v in _L1_xattn_all.items() if k in ('Wq', 'Wk', 'Wv', 'Wo', 'bo', 'token_indices_A', 'token_indices_B')}
    del _L1_xattn_all

    def _L2_xattn_setup():
        import jax, jax.numpy as jnp
        import numpy as np
        D_MODEL = 128
        N_HEADS = 16
        N_KV_HEADS = 4
        HEAD_DIM = D_MODEL // N_HEADS
        SPEAKER_DIM = 256
        EPS = 1e-05

        def rmsnorm(x, w, eps=EPS):
            xf = x.astype(jnp.float32)
            inv = jax.lax.rsqrt(jnp.mean(xf * xf, axis=-1, keepdims=True) + eps)
            return (xf * inv).astype(x.dtype) * w
        key = jax.random.key(seed)
        ks = jax.random.split(key, 7)
        B, T, S = (4, 256, 64)
        x = jax.random.normal(ks[0], (B, T, D_MODEL), dtype=jnp.float32)
        cond = jax.random.normal(ks[1], (B, S, SPEAKER_DIM), dtype=jnp.float32)
        sq = 0.02
        wq = jax.random.normal(ks[2], (D_MODEL, N_HEADS * HEAD_DIM), dtype=jnp.float32) * sq
        wk = jax.random.normal(ks[3], (SPEAKER_DIM, N_KV_HEADS * HEAD_DIM), dtype=jnp.float32) * sq
        wv = jax.random.normal(ks[4], (SPEAKER_DIM, N_KV_HEADS * HEAD_DIM), dtype=jnp.float32) * sq
        wo = jax.random.normal(ks[5], (N_HEADS * HEAD_DIM, D_MODEL), dtype=jnp.float32) * sq
        norm_w = jnp.ones((D_MODEL,), dtype=jnp.float32)
        return {'x': x, 'cond': cond, 'wq': wq, 'wk': wk, 'wv': wv, 'wo': wo, 'norm_w': norm_w}
    _L2_xattn_all = _L2_xattn_setup()
    _L2_xattn_in = {k: v for k, v in _L2_xattn_all.items() if k in ('wq', 'wk', 'wv', 'wo', 'norm_w')}
    del _L2_xattn_all

    def _L3_xattn_setup():
        import jax, jax.numpy as jnp
        import numpy as np
        HEADS = 16
        HEAD_DIM = 64
        SUPPRESS = 20.0
        key = jax.random.key(seed)
        ks = jax.random.split(key, 8)
        B, HW, C, T, CT = (8, 512, 128, 77, 256)
        inner = HEADS * HEAD_DIM
        scale = 0.02
        return {'hidden_states': jax.random.normal(ks[0], (B, HW, C), jnp.float32), 'encoder_hidden_states': jax.random.normal(ks[1], (B, T, CT), jnp.float32), 'mask_A': (jax.random.uniform(ks[2], (HW,)) > 0.5).astype(jnp.float32), 'mask_B': (jax.random.uniform(ks[3], (HW,)) > 0.5).astype(jnp.float32), 'Wq': jax.random.normal(ks[4], (C, inner), jnp.float32) * scale, 'Wk': jax.random.normal(ks[5], (CT, inner), jnp.float32) * scale, 'Wv': jax.random.normal(ks[6], (CT, inner), jnp.float32) * scale, 'Wo': jax.random.normal(ks[7], (inner, C), jnp.float32) * scale, 'bo': jnp.zeros((C,), jnp.float32), 'token_indices_A': jnp.array([2, 3], dtype=jnp.int64), 'token_indices_B': jnp.array([5, 6], dtype=jnp.int64)}
    _L3_xattn_all = _L3_xattn_setup()
    _L3_xattn_in = {k: v for k, v in _L3_xattn_all.items() if k in ('Wq', 'Wk', 'Wv', 'Wo', 'bo', 'token_indices_A', 'token_indices_B')}
    del _L3_xattn_all
    return {'x': x, 'ctx_2048': ctx_2048, 'mask_S_fk1': mask_S_fk1, 'mask_S_fk0': mask_S_fk0, 'L0_xattn_Wq': _L0_xattn_in['Wq'], 'L0_xattn_Wk': _L0_xattn_in['Wk'], 'L0_xattn_Wv': _L0_xattn_in['Wv'], 'L0_xattn_Wo': _L0_xattn_in['Wo'], 'L0_xattn_bo': _L0_xattn_in['bo'], 'L0_xattn_token_indices_A': _L0_xattn_in['token_indices_A'], 'L0_xattn_token_indices_B': _L0_xattn_in['token_indices_B'], 'L1_xattn_Wq': _L1_xattn_in['Wq'], 'L1_xattn_Wk': _L1_xattn_in['Wk'], 'L1_xattn_Wv': _L1_xattn_in['Wv'], 'L1_xattn_Wo': _L1_xattn_in['Wo'], 'L1_xattn_bo': _L1_xattn_in['bo'], 'L1_xattn_token_indices_A': _L1_xattn_in['token_indices_A'], 'L1_xattn_token_indices_B': _L1_xattn_in['token_indices_B'], 'L2_xattn_wq': _L2_xattn_in['wq'], 'L2_xattn_wk': _L2_xattn_in['wk'], 'L2_xattn_wv': _L2_xattn_in['wv'], 'L2_xattn_wo': _L2_xattn_in['wo'], 'L2_xattn_norm_w': _L2_xattn_in['norm_w'], 'L3_xattn_Wq': _L3_xattn_in['Wq'], 'L3_xattn_Wk': _L3_xattn_in['Wk'], 'L3_xattn_Wv': _L3_xattn_in['Wv'], 'L3_xattn_Wo': _L3_xattn_in['Wo'], 'L3_xattn_bo': _L3_xattn_in['bo'], 'L3_xattn_token_indices_A': _L3_xattn_in['token_indices_A'], 'L3_xattn_token_indices_B': _L3_xattn_in['token_indices_B']}

def reference(x, ctx_2048, mask_S_fk1, mask_S_fk0, L0_xattn_Wq, L0_xattn_Wk, L0_xattn_Wv, L0_xattn_Wo, L0_xattn_bo, L0_xattn_token_indices_A, L0_xattn_token_indices_B, L1_xattn_Wq, L1_xattn_Wk, L1_xattn_Wv, L1_xattn_Wo, L1_xattn_bo, L1_xattn_token_indices_A, L1_xattn_token_indices_B, L2_xattn_wq, L2_xattn_wk, L2_xattn_wv, L2_xattn_wo, L2_xattn_norm_w, L3_xattn_Wq, L3_xattn_Wk, L3_xattn_Wv, L3_xattn_Wo, L3_xattn_bo, L3_xattn_token_indices_A, L3_xattn_token_indices_B):
    import jax
    import jax.numpy as jnp

    def _L0_xattn_ref(hidden_states, encoder_hidden_states, mask_A, mask_B, Wq, Wk, Wv, Wo, bo, token_indices_A, token_indices_B):
        import jax, jax.numpy as jnp
        import numpy as np
        HEADS = 16
        HEAD_DIM = 64
        SUPPRESS = 20.0
        B, HW, C = hidden_states.shape
        T = encoder_hidden_states.shape[1]
        residual = hidden_states
        q = hidden_states @ Wq
        k = encoder_hidden_states @ Wk
        v = encoder_hidden_states @ Wv
        q = q.reshape(B, HW, HEADS, HEAD_DIM).transpose(0, 2, 1, 3)
        k = k.reshape(B, T, HEADS, HEAD_DIM).transpose(0, 2, 1, 3)
        v = v.reshape(B, T, HEADS, HEAD_DIM).transpose(0, 2, 1, 3)
        scale = HEAD_DIM ** (-0.5)
        logits = jnp.einsum('bhqd,bhkd->bhqk', q, k) * scale
        suppress_A_in = 1.0 - mask_A
        suppress_B_in = 1.0 - mask_B
        col_bias = jnp.zeros((HW, T), logits.dtype)
        col_bias = col_bias.at[:, token_indices_A].set((-SUPPRESS * suppress_A_in)[:, None])
        col_bias = col_bias.at[:, token_indices_B].set((-SUPPRESS * suppress_B_in)[:, None])
        logits = logits + col_bias[None, None, :, :]
        probs = jax.nn.softmax(logits, axis=-1)
        out = jnp.einsum('bhqk,bhkd->bhqd', probs, v)
        out = out.transpose(0, 2, 1, 3).reshape(B, HW, HEADS * HEAD_DIM)
        out = out @ Wo + bo
        out = out + residual
        return out

    def _L1_xattn_ref(hidden_states, encoder_hidden_states, mask_A, mask_B, Wq, Wk, Wv, Wo, bo, token_indices_A, token_indices_B):
        import jax, jax.numpy as jnp
        import numpy as np
        HEADS = 16
        HEAD_DIM = 64
        SUPPRESS = 20.0
        B, HW, C = hidden_states.shape
        T = encoder_hidden_states.shape[1]
        residual = hidden_states
        q = hidden_states @ Wq
        k = encoder_hidden_states @ Wk
        v = encoder_hidden_states @ Wv
        q = q.reshape(B, HW, HEADS, HEAD_DIM).transpose(0, 2, 1, 3)
        k = k.reshape(B, T, HEADS, HEAD_DIM).transpose(0, 2, 1, 3)
        v = v.reshape(B, T, HEADS, HEAD_DIM).transpose(0, 2, 1, 3)
        scale = HEAD_DIM ** (-0.5)
        logits = jnp.einsum('bhqd,bhkd->bhqk', q, k) * scale
        suppress_A_in = 1.0 - mask_A
        suppress_B_in = 1.0 - mask_B
        col_bias = jnp.zeros((HW, T), logits.dtype)
        col_bias = col_bias.at[:, token_indices_A].set((-SUPPRESS * suppress_A_in)[:, None])
        col_bias = col_bias.at[:, token_indices_B].set((-SUPPRESS * suppress_B_in)[:, None])
        logits = logits + col_bias[None, None, :, :]
        probs = jax.nn.softmax(logits, axis=-1)
        out = jnp.einsum('bhqk,bhkd->bhqd', probs, v)
        out = out.transpose(0, 2, 1, 3).reshape(B, HW, HEADS * HEAD_DIM)
        out = out @ Wo + bo
        out = out + residual
        return out

    def _L2_xattn_ref(x, cond, wq, wk, wv, wo, norm_w):
        import jax, jax.numpy as jnp
        import numpy as np
        D_MODEL = 128
        N_HEADS = 16
        N_KV_HEADS = 4
        HEAD_DIM = D_MODEL // N_HEADS
        SPEAKER_DIM = 256
        EPS = 1e-05

        def rmsnorm(x, w, eps=EPS):
            xf = x.astype(jnp.float32)
            inv = jax.lax.rsqrt(jnp.mean(xf * xf, axis=-1, keepdims=True) + eps)
            return (xf * inv).astype(x.dtype) * w
        B, T, _ = x.shape
        S = cond.shape[1]
        n_rep = N_HEADS // N_KV_HEADS
        residual = x
        xn = rmsnorm(x, norm_w)
        q = (xn @ wq).reshape(B, T, N_HEADS, HEAD_DIM)
        k = (cond @ wk).reshape(B, S, N_KV_HEADS, HEAD_DIM)
        v = (cond @ wv).reshape(B, S, N_KV_HEADS, HEAD_DIM)
        qg = q.reshape(B, T, N_KV_HEADS, n_rep, HEAD_DIM)
        scale = 1.0 / np.sqrt(HEAD_DIM).astype(np.float32)
        scores = jnp.einsum('btgrd,bsgd->bgrts', qg, k) * scale
        attn = jax.nn.softmax(scores.astype(jnp.float32), axis=-1).astype(q.dtype)
        out = jnp.einsum('bgrts,bsgd->btgrd', attn, v).reshape(B, T, N_HEADS * HEAD_DIM)
        return residual + out @ wo

    def _L3_xattn_ref(hidden_states, encoder_hidden_states, mask_A, mask_B, Wq, Wk, Wv, Wo, bo, token_indices_A, token_indices_B):
        import jax, jax.numpy as jnp
        import numpy as np
        HEADS = 16
        HEAD_DIM = 64
        SUPPRESS = 20.0
        B, HW, C = hidden_states.shape
        T = encoder_hidden_states.shape[1]
        residual = hidden_states
        q = hidden_states @ Wq
        k = encoder_hidden_states @ Wk
        v = encoder_hidden_states @ Wv
        q = q.reshape(B, HW, HEADS, HEAD_DIM).transpose(0, 2, 1, 3)
        k = k.reshape(B, T, HEADS, HEAD_DIM).transpose(0, 2, 1, 3)
        v = v.reshape(B, T, HEADS, HEAD_DIM).transpose(0, 2, 1, 3)
        scale = HEAD_DIM ** (-0.5)
        logits = jnp.einsum('bhqd,bhkd->bhqk', q, k) * scale
        suppress_A_in = 1.0 - mask_A
        suppress_B_in = 1.0 - mask_B
        col_bias = jnp.zeros((HW, T), logits.dtype)
        col_bias = col_bias.at[:, token_indices_A].set((-SUPPRESS * suppress_A_in)[:, None])
        col_bias = col_bias.at[:, token_indices_B].set((-SUPPRESS * suppress_B_in)[:, None])
        logits = logits + col_bias[None, None, :, :]
        probs = jax.nn.softmax(logits, axis=-1)
        out = jnp.einsum('bhqk,bhkd->bhqd', probs, v)
        out = out.transpose(0, 2, 1, 3).reshape(B, HW, HEADS * HEAD_DIM)
        out = out @ Wo + bo
        out = out + residual
        return out
    x = _L0_xattn_ref(x, ctx_2048, mask_S_fk1, mask_S_fk0, L0_xattn_Wq, L0_xattn_Wk, L0_xattn_Wv, L0_xattn_Wo, L0_xattn_bo, L0_xattn_token_indices_A, L0_xattn_token_indices_B)
    x = _L1_xattn_ref(x, ctx_2048, mask_S_fk1, mask_S_fk0, L1_xattn_Wq, L1_xattn_Wk, L1_xattn_Wv, L1_xattn_Wo, L1_xattn_bo, L1_xattn_token_indices_A, L1_xattn_token_indices_B)
    x = _L2_xattn_ref(x, ctx_2048, L2_xattn_wq, L2_xattn_wk, L2_xattn_wv, L2_xattn_wo, L2_xattn_norm_w)
    x = _L3_xattn_ref(x, ctx_2048, mask_S_fk1, mask_S_fk0, L3_xattn_Wq, L3_xattn_Wk, L3_xattn_Wv, L3_xattn_Wo, L3_xattn_bo, L3_xattn_token_indices_A, L3_xattn_token_indices_B)
    return x

_drawn_inputs = setup_inputs


def setup_inputs(seed=0):
    import zlib

    import numpy as np

    out = dict(_drawn_inputs(seed))
    spreads = {'L0_xattn_bo': (0.0, 0.1),
     'L1_xattn_bo': (0.0, 0.1),
     'L2_xattn_norm_w': (1.0, 0.6),
     'L3_xattn_bo': (0.0, 0.1)}
    factors = {'mask_S_fk1': 8.0,
     'mask_S_fk0': 8.0,
     'L0_xattn_Wq': 8.0,
     'L0_xattn_Wk': 8.0,
     'L1_xattn_Wq': 8.0,
     'L1_xattn_Wk': 8.0,
     'L2_xattn_wq': 8.0,
     'L2_xattn_wk': 8.0,
     'L3_xattn_Wq': 8.0,
     'L3_xattn_Wk': 8.0}
    for name, (base, spread) in spreads.items():
        noise = np.random.default_rng([zlib.crc32(name.encode()), seed]).standard_normal(out[name].shape)
        drawn = base * np.exp(spread * noise) if base else spread * noise
        out[name] = jnp.asarray(drawn.astype(out[name].dtype))
    for name, factor in factors.items():
        out[name] = (out[name] * factor).astype(out[name].dtype)
    return out
```

```python
from contextlib import ExitStack

import concourse.bass as bass
from concourse import mybir

F32 = mybir.dt.float32
F32R = mybir.dt.float32r
ALU = mybir.AluOpType
ACT = mybir.ActivationFunctionType
AX = mybir.AxisListType

P = 128
B, T, C = 16, 128, 128
CT, KT = 256, 2
HEADS, HD = 16, 64
INNER = HEADS * HD
PAIRS = HEADS // 2
KV, RD = 4, 8
REP = HEADS // KV
GB = 2
G = B // GB
GT = GB * T
SLOTS = 8
SUPPRESS = 20.0
EPS = 1e-5
FAR = 3.4e38
CHUNK = 3 * 256
WV0 = 4 * CHUNK
WCOLS = WV0 + KT * INNER
WIDE = 3
NARROW_AT = 2 * G
LAST_AT = 3 * G


def build_program(nc, x, ctx_in, masks, tokens, wq, wk, wv, wo, bo, nwq, nwk, nwv, nwo, nw, out):
    with ExitStack() as stack:
        def sb(name, shape, dt=F32):
            return stack.enter_context(nc.sbuf_tensor(name, shape, dt))

        def sem(name):
            return stack.enter_context(nc.semaphore(name))

        xT = sb("xT", [P, B * T])
        xs_h, xs_l = sb("xs_h", [P, GT], F32R), sb("xs_l", [P, GT], F32R)
        c_h, c_l = sb("c_h", [P, KT, B * T], F32R), sb("c_l", [P, KT, B * T], F32R)
        cv_h, cv_l = sb("cv_h", [P, GB, KT, T], F32R), sb("cv_l", [P, GB, KT, T], F32R)
        w_h, w_l = sb("w_h", [P, WCOLS], F32R), sb("w_l", [P, WCOLS], F32R)
        w_raw = sb("w_raw", [P, WCOLS])
        wo_sb = sb("wo_sb", [P, PAIRS, C])
        k_h, k_l = sb("k_h", [P, PAIRS, 2, GT], F32R), sb("k_l", [P, PAIRS, 2, GT], F32R)
        q_h, q_l = sb("q_h", [P, PAIRS, GT], F32R), sb("q_l", [P, PAIRS, GT], F32R)
        v_sb = sb("v_sb", [P, GB, INNER])
        oT = sb("oT", [P, PAIRS, GT])
        probs = sb("probs", [P, 4, 4, T])
        probsT = sb("probsT", [P, 2, 4, T])
        nmax = sb("nmax", [P, 4, 4])
        den = sb("den", [P, 4, 4])
        rden = sb("rden", [P, 4, 4])
        ident = sb("ident", [P, P])
        mean_w = sb("mean_w", [P, P])
        alpha = sb("alpha", [P, T], F32R)
        sel = sb("sel", [P, WIDE, T], F32R)
        bias = sb("bias", [P, WIDE, T])
        bo_sb = sb("bo_sb", [P, WIDE])
        nw_sb = sb("nw_sb", [P, 1])
        eps_sb = sb("eps_sb", [P, 1])
        nw_h, nw_l = sb("nw_h", [P, 8, P], F32R), sb("nw_l", [P, 8, P], F32R)
        nwo_sb = sb("nwo_sb", [P, REP, C])
        gate = sb("gate", [P, 1])
        mrow = sb("mrow", [64, T])
        mhi = sb("mhi", [64, T], F32R)
        idx_i = sb("idx_i", [64, WIDE, 4], mybir.dt.int32)
        idx_f = sb("idx_f", [64, WIDE, 2, 4])
        flag = sb("flag", [64, 1])
        iota_i = sb("iota_i", [64, T], mybir.dt.int32)
        iota_f = sb("iota_f", [64, T])
        picked = sb("picked", [64, 2, T])
        both = sb("both", [64, T])

        x_raw = oT[:].rearrange("p a t -> p (a t)")
        ctx_raw = [v_sb[:].rearrange("p b n -> p (b n)"), probs[:].rearrange("p r h t -> p (r h t)")]
        nw_raw = probsT[:].rearrange("p r h t -> p (r h t)").rearrange("p (m n) -> p m n", m=8)
        k_hf, k_lf = (k[:].rearrange("p a s t -> p (a s t)") for k in (k_h, k_l))
        q_hf, q_lf = (q[:].rearrange("p a t -> p (a t)") for q in (q_h, q_l))
        nk_h, nk_l = ([k[:, e * KV * GT:(e + 1) * KV * GT].rearrange("p (g t) -> p g t", g=KV) for e in range(2)]
                      for k in (k_hf, k_lf))
        XN0 = 2 * KV * GT
        nq_h, nq_l = ([q[:, e * REP * GT:(e + 1) * REP * GT].rearrange("p (r t) -> p r t", r=REP)
                       for e in range(2)] for q in (q_hf, q_lf))
        nv = [v_sb[:, e, 0:GB * P].rearrange("p (b n) -> p b n", b=GB) for e in range(2)]
        noT = [oT[:, e * REP:(e + 1) * REP, :] for e in range(2)]

        def bank(name):
            return stack.enter_context(nc.psum_tensor(name, [P, 512], F32))

        ps_s = [bank("ps_s0"), bank("ps_s1")]
        ps_t = bank("ps_t")
        ps_o = bank("ps_o")
        ps_k = [bank("ps_k0"), bank("ps_k1")]
        ps_q = bank("ps_q")
        ps_v = bank("ps_v")
        setup_banks = [ps_s[0], ps_s[1], ps_k[0], ps_k[1], ps_q, ps_v]

        scores_ready = sem("scores_ready")
        max_ready = sem("max_ready")
        exp_done = sem("exp_done")
        rden_ready = sem("rden_ready")
        norm_done = sem("norm_done")
        pt_ready = sem("pt_ready")
        pt_copied = sem("pt_copied")
        o_ready = sem("o_ready")
        o_copied = sem("o_copied")
        k_ready, k_hi, k_lo = sem("k_ready"), sem("k_hi"), sem("k_lo")
        q_ready, q_hi, q_lo = sem("q_ready"), sem("q_hi"), sem("q_lo")
        v_ready, v_copied = sem("v_ready"), sem("v_copied")
        nk_ready, nk_hi, nk_lo = sem("nk_ready"), sem("nk_hi"), sem("nk_lo")
        nq_ready, nq_hi, nq_lo = sem("nq_ready"), sem("nq_hi"), sem("nq_lo")
        nv_ready, nv_copied = sem("nv_ready"), sem("nv_copied")
        y_ready, x_updated = sem("y_ready"), sem("x_updated")
        xs_hi, xs_lo = sem("xs_hi"), sem("xs_lo")
        cv_loaded = [sem("cv_loaded0"), sem("cv_loaded1")]
        w_loaded = sem("w_loaded")
        w_hi, w_lo = sem("w_hi"), sem("w_lo")
        wo_loaded = sem("wo_loaded")
        x_loaded = sem("x_loaded")
        ctx_loaded = [sem("ctx_loaded0"), sem("ctx_loaded1")]
        small_loaded, columns_loaded = sem("small_loaded"), sem("columns_loaded")
        narrow_loaded = sem("narrow_loaded")
        zeroed = sem("zeroed")
        ident_ready = sem("ident_ready")
        setup_t, setup_hi, setup_lo = sem("setup_t"), sem("setup_hi"), sem("setup_lo")
        rows_step, rows_ready, bias_made, bias_ready = (sem("rows_step"), sem("rows_ready"), sem("bias_made"),
                                                        sem("bias_ready"))
        nw_hi, nw_lo = sem("nw_hi"), sem("nw_lo")
        k_cleared = sem("k_cleared")
        sq_ready, mean_ready, root_ready, inv_ready = (sem("sq_ready"), sem("mean_ready"), sem("root_ready"),
                                                       sem("inv_ready"))
        xn_ready, xn_hi, xn_lo = sem("xn_ready"), sem("xn_hi"), sem("xn_lo")
        fin_t, fin_copied, stored = sem("fin_t"), sem("fin_copied"), sem("stored")

        def wait(eng, semaphore, value):
            if not isinstance(value, int) or value > 0:
                eng.wait_ge(semaphore, value)

        PIECES = {0: [("k", 3, 0), ("v", 0, 0)], 1: [("k", 0, 1), ("q", 2, 0)], 2: [("y", 0, 0)],
                  3: [("v", 1, 0), ("q", 3, 0)], 4: [("y", 1, 0)], 5: [("q", 0, 1), ("v", 2, 0)],
                  6: [("k", 1, 1), ("v", 3, 0)], 7: [("k", 2, 1), ("q", 1, 1)]}
        Y_AT = [u for u in range(SLOTS) if PIECES[u][0][0] == "y"]
        FIRST_PIECES = [("k", 0), ("q", 0), ("k", 1), ("q", 1), ("k", 2)]
        K_BANK = {("k", 3): 0, ("k", 0): 1, ("y", 0): 0, ("y", 1): 1, ("k", 1): 0, ("k", 2): 1}
        NPIECES = {2: [("y", 0, 0)], 3: [("q", 0, 1)], 4: [("y", 1, 0)], 5: [("q", 1, 1)], 6: [("k", 0, 1)],
                   7: [("v", 0, 1)]}
        TLAG, PLAG = 2, 3
        REFRESH = {0: [0], 1: [1], 2: [2], 4: [3], 5: [4], 7: [5]}

        def chunk(t, c):
            if c < 4:
                return t[:, c * CHUNK:(c + 1) * CHUNK]
            n = KT * INNER // 2
            return t[:, WV0 + (c - 4) * n:WV0 + (c - 3) * n]

        def step_cols(g):
            return bass.ds(g * GT, GT)

        block = stack.enter_context(nc.Block())

        @block.sync
        def _(sp):
            def load_weights(layer):
                for c in range(4):
                    cols = slice(256 * c, 256 * c + 256)
                    dst = chunk(w_raw, c).rearrange("p (m n) -> p m n", m=3)
                    sp.dma_start(dst[:, 0:KT, :],
                                 wk[layer].rearrange("(k p) n -> p k n", p=P)[:, :, cols]).then_inc(w_loaded, 16)
                    sp.dma_start(dst[:, KT, :], wq[layer, :, cols]).then_inc(w_loaded, 16)
                for c in range(2):
                    sp.dma_start(chunk(w_raw, 4 + c).rearrange("p (k n) -> p k n", k=KT),
                                 wv[layer].rearrange("(k p) n -> p k n", p=P)[:, :, 512 * c:512 * c + 512])\
                      .then_inc(w_loaded, 16)

            def load_wo(layer):
                sp.dma_start(wo_sb[:, :, :], wo[layer].rearrange("(a p) n -> p a n", p=P)).then_inc(wo_loaded, 16)

            def load_cv(g, b, after):
                if after is not None:
                    wait(sp, after[0], after[1])
                for dst, src in ((cv_h, c_h), (cv_l, c_l)):
                    sp.dma_start(dst[:, b, :, :].bitcast(F32), src[:, :, bass.ds(g * GT + b * T, T)].bitcast(F32))\
                      .then_inc(cv_loaded[b], 16)

            sp.wait_ge(zeroed, 2)
            for base in (0, 32):
                sp.dma_start(mrow[base:base + 2, :], masks).then_inc(small_loaded, 16)
                sp.dma_start(idx_i[base:base + 2, :, 0:2], tokens.rearrange("l r c -> r l c"))\
                  .then_inc(small_loaded, 16)
                for r in range(2):
                    sp.dma_start(idx_i[base + r:base + r + 1, :, 2:4],
                                 tokens[:, 1:2, :].rearrange("l r c -> r l c")).then_inc(small_loaded, 16)
            for h in range(2):
                sp.dma_start(ctx_raw[h].rearrange("p (b c) -> p b c", c=CT),
                             ctx_in[8 * h:8 * h + 8].rearrange("b t c -> t b c")).then_inc(ctx_loaded[h], 16)
            load_weights(0)
            load_wo(0)
            sp.dma_start(bo_sb[:, :], bo).then_inc(columns_loaded, 16)
            sp.dma_start(nw_sb[:, :], nw).then_inc(columns_loaded, 16)
            sp.wait_ge(zeroed, 4)
            for r in range(REP):
                sp.dma_start(nw_raw[:, r, :].rearrange("p (g d) -> p g d", g=KV)[:, :, 0:RD],
                             nwq.rearrange("p (g r d) -> p g r d", g=KV, r=REP)[:, :, r, :])\
                  .then_inc(narrow_loaded, 16)
                for g in range(KV):
                    h = g * REP + r
                    sp.dma_start(nwo_sb[32 * g:32 * g + RD, r, :], nwo[h * RD:(h + 1) * RD, :])\
                      .then_inc(narrow_loaded, 16)
            for i, w in enumerate((nwk, nwv)):
                for k in range(KT):
                    sp.dma_start(nw_raw[:, 4 + 2 * i + k, :].rearrange("p (g d) -> p g d", g=KV)[:, :, 0:RD],
                                 w[k * P:(k + 1) * P, :].rearrange("p (g d) -> p g d", g=KV))\
                      .then_inc(narrow_loaded, 16)

            sp.wait_ge(setup_hi, 12)
            sp.wait_ge(setup_lo, 8)
            for b in range(GB):
                load_cv(0, b, None)
            sp.wait_ge(w_hi, 6)
            sp.wait_ge(w_lo, 6)
            load_weights(1)
            with sp.Fori(1, G) as s:
                for b in range(GB):
                    load_cv(s, b, (v_ready, 4 * s - 1 + b))
            for b in range(GB):
                load_cv(0, b, (v_ready, 4 * G - 1 + b))
            sp.wait_ge(y_ready, 2 * G)
            load_wo(1)
            sp.wait_ge(w_hi, 12)
            sp.wait_ge(w_lo, 12)
            load_weights(2)
            with sp.Fori(G + 1, 2 * G) as s:
                for b in range(GB):
                    load_cv(s - G, b, (v_ready, 4 * s - 1 + b))
            for b in range(GB):
                load_cv(0, b, (v_ready, 8 * G - 1 + b))
            sp.wait_ge(y_ready, 4 * G)
            load_wo(2)
            with sp.Fori(1, G) as g:
                for b in range(GB):
                    load_cv(g, b, (nv_ready, g))
            for b in range(GB):
                load_cv(0, b, (nv_ready, G))
            with sp.Fori(2 * G + 1, 3 * G) as s:
                for b in range(GB):
                    load_cv(s - 2 * G, b, (v_ready, 4 * s - 1 + b))
            for q in range(4):
                sp.wait_ge(fin_copied, q + 1)
                sp.dma_start(out[4 * q:4 * q + 4].rearrange("b t c -> t b c"),
                             probs[:, q, :, :]).then_inc(stored, 16)
            sp.wait_ge(stored, 64)

        @block.gpsimd
        def _(pool):
            pool.memset(mrow[:, :], 0.0).then_inc(zeroed, 1)
            pool.memset(idx_i[:, :, :], 0).then_inc(zeroed, 1)
            pool.memset(nw_raw, 0.0).then_inc(zeroed, 1)
            pool.memset(nwo_sb[:, :, :], 0.0).then_inc(zeroed, 1)
            pool.memset(ident[:, :], 0.0).then_inc(zeroed, 1)
            pool.wait_ge(zeroed, 5)
            pool.affine_select(out=ident[:, :], in_=ident[:, :], compare_op=ALU.not_equal, fill=1.0, base=0,
                               pattern=[[-1, P]], channel_multiplier=1).then_inc(ident_ready, 1)
            pool.iota(iota_i[:, :], pattern=[[1, T]], base=0, channel_multiplier=0).then_inc(ident_ready, 1)
            pool.memset(mean_w[:, :], 1.0 / C).then_inc(ident_ready, 1)

            pool.wait_ge(ident_ready, 3)
            cleared = [0]

            def clear(ap):
                cleared[0] += 1
                pool.memset(ap.bitcast(F32), 0.0).then_inc(k_cleared, 1)
                pool.wait_ge(k_cleared, cleared[0])

            def zero_k():
                for k in (k_h, k_l):
                    clear(k[64:128, :, 0, :])
                    clear(k[0:64, :, 1, :])

            zero_k()

            def norm(n, ring):
                wait(pool, rden_ready, n + 1)
                p = probs[:, ring, :, :]
                pool.tensor_tensor(p, p, rden[:, ring, :].unsqueeze(2).to_broadcast([P, 4, T]), ALU.mult)\
                    .then_inc(norm_done, 1)

            def steps(first, last):
                with pool.Fori(first, last) as t:
                    for u in range(SLOTS):
                        norm(8 * t + u, u % 4)

            steps(0, NARROW_AT)
            pool.wait_ge(x_updated, 2 * NARROW_AT)
            pool.wait_ge(scores_ready, 8 * NARROW_AT)
            for k in (k_hf, k_lf):
                clear(k[:, 0:XN0])
            steps(NARROW_AT, LAST_AT)
            pool.wait_ge(scores_ready, 8 * LAST_AT)
            pool.wait_ge(nq_ready, 2 * G)
            pool.wait_ge(norm_done, 8 * LAST_AT)
            zero_k()
            steps(LAST_AT, 4 * G)

        @block.tensor
        def _(pe):
            def three(out_ap, lhs, rhs, first, last):
                (a_h, a_l), (b_h, b_l) = lhs, rhs
                pe.matmul(out_ap, a_h, b_l, start=first, stop=False, skip_group_check=True)
                pe.matmul(out_ap, a_l, b_h, start=False, stop=False, skip_group_check=True)
                return pe.matmul(out_ap, a_h, b_h, start=False, stop=last, skip_group_check=True)

            pe.wait_ge(ident_ready, 1)
            for i in range(12):
                if i == 0:
                    pe.wait_ge(ctx_loaded[0], 16)
                elif i == 4:
                    pe.wait_ge(ctx_loaded[1], 16)
                elif i == 8:
                    pe.wait_ge(x_loaded, 16)
                if i >= 6:
                    pe.wait_ge(setup_hi, i - 5)
                    pe.wait_ge(setup_lo, i - 5)
                for j in range(4):
                    if i < 8:
                        b, k = 4 * (i // 2) + j, i % 2
                        src = ctx_raw[b // 8][:, (b % 8) * CT + k * P:(b % 8) * CT + (k + 1) * P]
                    else:
                        b = 4 * (i - 8) + j
                        src = x_raw[:, b * C:(b + 1) * C]
                    mm = pe.transpose(setup_banks[i % 6][:, j * P:(j + 1) * P], src, ident[:, :])
                mm.then_inc(setup_t, 1)

            pe.wait_ge(rows_ready, 1)
            pe.matmul(ps_t[:, 0:WIDE * T], alpha[:, :], sel[:, :, :].rearrange("p l t -> p (l t)"), start=True,
                      stop=True).then_inc(bias_made, 1)

            def k_piece(s, g, jj, weights):
                idx = 4 * s + jj
                if weights is not None:
                    pe.wait_ge(w_hi, weights)
                    pe.wait_ge(w_lo, weights)
                wait(pe, k_hi, idx - 1)
                wait(pe, k_lo, idx - 1)
                dst = ps_k[K_BANK["k", jj]]
                for p in range(2):
                    for k in range(KT):
                        at = jj * CHUNK + k * 256 + p * P
                        mm = three(dst[:, p * GT:(p + 1) * GT],
                                   (w_h[:, at:at + P], w_l[:, at:at + P]),
                                   (c_h[:, k, step_cols(g)], c_l[:, k, step_cols(g)]), k == 0, k == KT - 1)
                mm.then_inc(k_ready, 1)

            def q_piece(s, jj, weights):
                idx = 4 * s + jj
                if weights is not None:
                    pe.wait_ge(w_hi, weights)
                    pe.wait_ge(w_lo, weights)
                wait(pe, q_hi, idx)
                wait(pe, q_lo, idx)
                wait(pe, xs_hi, s + 1)
                wait(pe, xs_lo, s + 1)
                for p in range(2):
                    at = jj * CHUNK + 2 * 256 + p * P
                    mm = three(ps_q[:, p * GT:(p + 1) * GT], (w_h[:, at:at + P], w_l[:, at:at + P]),
                               (xs_h[:, :], xs_l[:, :]), True, True)
                mm.then_inc(q_ready, 1)

            def v_piece(s, i, weights, cv):
                b, half = i % 2, i // 2
                if weights is not None:
                    pe.wait_ge(w_hi, weights)
                    pe.wait_ge(w_lo, weights)
                wait(pe, v_copied, 4 * s + i)
                wait(pe, cv_loaded[b], cv)
                for k in range(KT):
                    at = WV0 + half * KT * 512 + k * 512
                    mm = three(ps_v[:, :], (cv_h[:, b, k, :], cv_l[:, b, k, :]),
                               (w_h[:, at:at + 512], w_l[:, at:at + 512]), k == 0, k == KT - 1)
                mm.then_inc(v_ready, 1)

            def y_piece(t, b, narrow, n_wo, last=False):
                wait(pe, o_copied, 8 * t - 1 + b)
                if narrow is not None or last:
                    wait(pe, x_updated, 2 * t - 3 + b)
                pe.wait_ge(wo_loaded, n_wo)
                dst = ps_k[K_BANK["y", b]][:, 0:T]
                if narrow is None:
                    for a in range(PAIRS):
                        mm = pe.matmul(dst, wo_sb[:, a, :], oT[:, a, b * T:(b + 1) * T], start=(a == 0),
                                       stop=(a == PAIRS - 1))
                else:
                    for r in range(REP):
                        mm = pe.matmul(dst, nwo_sb[:, r, :], noT[narrow][:, r, b * T:(b + 1) * T],
                                       start=(r == 0), stop=(r == REP - 1))
                mm.then_inc(y_ready, 1)

            def transposes(n, u):
                wait(pe, norm_done, n + 1)
                wait(pe, pt_copied, n)
                for h in range(4):
                    mm = pe.transpose(ps_t[:, h * T:(h + 1) * T], probs[:, u % 4, h, :], ident[:, :])
                mm.then_inc(pt_ready, 1)

            def weigh(n, u, narrow):
                wait(pe, pt_copied, n + 1)
                wait(pe, o_copied, n)
                jj, b = u // 2, u % 2
                for h in range(4):
                    if narrow is None:
                        a, p = h % 2, h // 2
                        at = (4 * jj + h) * HD
                        mm = pe.matmul(ps_o[a * HD:(a + 1) * HD, p * T:(p + 1) * T], v_sb[:, b, at:at + HD],
                                       probsT[:, u % 2, h, :], start=True, stop=True)
                    else:
                        mm = pe.matmul(ps_o[32 * h:32 * h + 32, 0:T], nv[narrow][:, b, 32 * h:32 * h + 32],
                                       probsT[:, u % 2, h, :], start=True, stop=True)
                mm.then_inc(o_ready, 1)

            def scores(n, s, u, layer):
                jj, b = u // 2, u % 2
                wait(pe, exp_done, n - 1)
                if b == 0:
                    for part in (k_hi, k_lo, q_hi, q_lo):
                        wait(pe, part, 4 * s + jj + 1)
                bk = ps_s[u % 2]
                for p in range(2):
                    pair, tok = 2 * jj + p, slice(b * T, (b + 1) * T)
                    mm = three(bk[:, p * 2 * T:(p + 1) * 2 * T].rearrange("p (h t) -> p h t", h=2),
                               (q_h[:, pair, tok], q_l[:, pair, tok]),
                               (k_h[:, pair, :, tok], k_l[:, pair, :, tok]), True, True)
                mm.then_inc(scores_ready, 1)

            def wide_step(t, s, g, layer, head=False, follow=True, fresh=False):
                gn = 0 if fresh else g + 1
                for u in range(SLOTS):
                    n = 8 * t + u
                    scores(n, s, u, layer)
                    if not (head and u < TLAG):
                        transposes(n - TLAG, (u - TLAG) % 8)
                    for what, i, ahead in PIECES[u]:
                        if ahead and not follow:
                            continue
                        new = None
                        if ahead and fresh:
                            new = 6 * (layer + 1) + i + 1
                        elif not ahead and isinstance(s, int) and s % G == 0 and what != "y":
                            new = 6 * layer + {"k": 4, "q": i + 1, "v": 5 + i // 2}[what]
                        if what == "k":
                            if i == 1 and not head:
                                wait(pe, x_updated, 2 * t - 1)
                            if i == 2 and not head:
                                wait(pe, x_updated, 2 * t)
                            k_piece(s + ahead, gn if ahead else g, i, new)
                        elif what == "q":
                            q_piece(s + ahead, i, new)
                        elif what == "v":
                            v_piece(s, i, new, 32 * (t + 1))
                        elif not head:
                            user = 4 * s + 4 + (i if follow else 0)
                            wait(pe, k_hi, user)
                            wait(pe, k_lo, user)
                            y_piece(t, i, None, 16 * layer if isinstance(s, int) and s % G == 0
                                    else 16 * (layer + 1))
                    if not (head and u < PLAG):
                        m = u - PLAG
                        wait(pe, v_copied, 4 * s + 2 * (m // 4) + m % 2 + 1 if m >= 0 else 4 * s)
                        weigh(n - PLAG, (u - PLAG) % 8, None)

            def flush(t, narrow, n_wo, n_v=0):
                wait(pe, v_copied, n_v)
                for m in (2, 1):
                    transposes(8 * t - m, 8 - m)
                    weigh(8 * t - m - 1, 7 - m, narrow)
                weigh(8 * t - 1, 7, narrow)
                for b in range(GB):
                    y_piece(t, b, narrow, n_wo, last=True)

            def first_pieces(s, layer):
                for what, i in FIRST_PIECES:
                    if what == "k":
                        k_piece(s, 0, i, 6 * layer + i + 1)
                    else:
                        q_piece(s, i, 6 * layer + i + 1)

            pe.wait_ge(setup_hi, 12)
            pe.wait_ge(setup_lo, 8)
            first_pieces(0, 0)
            pe.wait_ge(k_cleared, 4)
            pe.wait_ge(bias_ready, 1)
            wide_step(0, 0, 0, 0, head=True)
            with pe.Fori(1, G - 1) as s:
                wide_step(s, s, s, 0)
            wide_step(G - 1, G - 1, G - 1, 0, fresh=True)
            wide_step(G, G, 0, 1)
            with pe.Fori(G + 1, 2 * G - 1) as s:
                wide_step(s, s, s - G, 1)
            wide_step(2 * G - 1, 2 * G - 1, G - 1, 1, follow=False)
            flush(2 * G, None, 32, 8 * G)

            def nk_piece(g, e):
                wait(pe, x_updated, 2 * (NARROW_AT + g) - 2)
                for k in range(KT):
                    mm = three(ps_k[1][:, 0:GT], (nw_h[:, 4 + k, :], nw_l[:, 4 + k, :]),
                               (c_h[:, k, step_cols(g)], c_l[:, k, step_cols(g)]), k == 0, k == KT - 1)
                mm.then_inc(nk_ready, 1)

            def nq_piece(g, half):
                wait(pe, nq_hi, 2 * g + half)
                wait(pe, nq_lo, 2 * g + half)
                cols = bass.ds(g * GT + XN0, GT)
                for i in range(2):
                    r = 2 * half + i
                    mm = three(ps_q[:, i * GT:(i + 1) * GT], (nw_h[:, r, :], nw_l[:, r, :]),
                               (k_hf[:, cols], k_lf[:, cols]), True, True)
                mm.then_inc(nq_ready, 1)

            def nv_piece(g):
                wait(pe, nv_copied, g)
                for b in range(GB):
                    wait(pe, cv_loaded[b], 32 * (NARROW_AT + g + 1))
                    for k in range(KT):
                        mm = three(ps_v[:, b * P:(b + 1) * P], (cv_h[:, b, k, :], cv_l[:, b, k, :]),
                                   (nw_h[:, 6 + k, :], nw_l[:, 6 + k, :]), k == 0, k == KT - 1)
                mm.then_inc(nv_ready, 1)

            def narrow_step(t, g, e, head=False, follow=True):
                for u in range(SLOTS):
                    n, r, b = 8 * t + u, u // 2, u % 2
                    wait(pe, exp_done, n - 1)
                    if u == 0:
                        wait(pe, nk_hi, g + 1)
                        wait(pe, nk_lo, g + 1)
                    if u in (0, 4):
                        wait(pe, nq_hi, 2 * g + u // 4 + 1)
                        wait(pe, nq_lo, 2 * g + u // 4 + 1)
                    tok = slice(b * T, (b + 1) * T)
                    three(ps_s[u % 2][:, :].rearrange("p (h t) -> p h t", h=4),
                          (nq_h[e][:, r, tok], nq_l[e][:, r, tok]),
                          (nk_h[e][:, :, tok], nk_l[e][:, :, tok]), True, True).then_inc(scores_ready, 1)
                    if not (head and u < TLAG):
                        transposes(n - TLAG, (u - TLAG) % 8)
                    for what, i, ahead in NPIECES.get(u, ()):
                        if what == "y":
                            if not head:
                                wait(pe, nk_hi, g + 1)
                                wait(pe, nk_lo, g + 1)
                                y_piece(t, i, 1 - e, 48)
                        elif follow:
                            {"k": lambda: nk_piece(g + 1, 1 - e), "q": lambda: nq_piece(g + 1, i),
                             "v": lambda: nv_piece(g + 1)}[what]()
                    if not (head and u < PLAG):
                        if u == PLAG:
                            wait(pe, nv_copied, g + 1)
                        weigh(n - PLAG, (u - PLAG) % 8, e if u >= PLAG else 1 - e)

            for i in range(4):
                pe.wait_ge(sq_ready, i + 1)
                pe.matmul([ps_s[0], ps_s[1], ps_q, ps_v][i][:, :], mean_w[:, :], probs[:, i, :, :],
                          start=True, stop=True).then_inc(mean_ready, 1)
            pe.wait_ge(nw_hi, 1)
            pe.wait_ge(nw_lo, 1)
            nk_piece(0, 0)
            pe.wait_ge(xn_hi, 4)
            pe.wait_ge(xn_lo, 4)
            nq_piece(0, 0)
            nq_piece(0, 1)
            nv_piece(0)
            narrow_step(NARROW_AT, 0, 0, head=True)
            narrow_step(NARROW_AT + 1, 1, 1)
            with pe.Fori(1, G // 2 - 1) as i:
                for e in range(2):
                    narrow_step(2 * i + (NARROW_AT + e), 2 * i + e, e)
            narrow_step(LAST_AT - 2, G - 2, 0)
            narrow_step(LAST_AT - 1, G - 1, 1, follow=False)
            flush(LAST_AT, 1, 48)

            pe.wait_ge(x_updated, 2 * LAST_AT)
            pe.wait_ge(nv_copied, G)
            first_pieces(2 * G, 2)
            pe.wait_ge(k_cleared, 10)
            wide_step(LAST_AT, 2 * G, 0, 2, head=True)
            with pe.Fori(1, G - 1) as g:
                wide_step(g + LAST_AT, g + 2 * G, g, 2)
            wide_step(4 * G - 1, 3 * G - 1, G - 1, 2, follow=False)
            flush(4 * G, None, 48, 12 * G)

            for q in range(4):
                pe.wait_ge(x_updated, 8 * G)
                pe.wait_ge(exp_done, 32 * G)
                for j in range(4):
                    b = 4 * q + j
                    mm = pe.transpose([ps_s[0], ps_s[1], ps_q, ps_v][q][:, j * P:(j + 1) * P],
                                      xT[:, b * T:(b + 1) * T], ident[:, :])
                mm.then_inc(fin_t, 1)

        @block.scalar
        def _(act):
            act.dma_start(x_raw.rearrange("p (b c) -> p b c", c=C), x.rearrange("b t c -> t b c"))\
               .then_inc(x_loaded, 16)
            for i in range(12):
                act.wait_ge(setup_t, i + 1)
                if i < 8:
                    dst = c_h[:, i % 2, 512 * (i // 2):512 * (i // 2) + 512]
                else:
                    dst = xT[:, 512 * (i - 8):512 * (i - 8) + 512]
                act.activation(dst, setup_banks[i % 6][:, :], ACT.Copy).then_inc(setup_hi, 1)

            def split(c, layer):
                act.wait_ge(w_loaded, 160 * (layer + 1))
                if layer:
                    s = G * layer - 1
                    if c < 4:
                        act.wait_ge(k_ready, 4 * s + c + 1)
                        act.wait_ge(q_ready, 4 * s + c + 1)
                    else:
                        act.wait_ge(v_ready, 4 * s + 2 * (c - 4) + 2)
                act.activation(chunk(w_h, c), chunk(w_raw, c), ACT.Copy).then_inc(w_hi, 1)

            def split_x(s, g, after):
                wait(act, q_ready, 4 * s)
                wait(act, x_updated, after)
                act.activation(xs_h[:, :], xT[:, step_cols(g)], ACT.Copy).then_inc(xs_hi, 1)

            def k_upper(s, jj):
                wait(act, k_ready, 4 * s + jj + 1)
                src = ps_k[K_BANK["k", jj]][:, :].rearrange("p (a t) -> p a t", a=2)
                for half in range(2):
                    rows = slice(64 * half, 64 * half + 64)
                    last = act.activation(k_h[rows, 2 * jj:2 * jj + 2, half, :], src[rows], ACT.Copy)
                last.then_inc(k_hi, 1)

            def q_upper(s, jj):
                wait(act, q_ready, 4 * s + jj + 1)
                act.activation(q_h[:, 2 * jj:2 * jj + 2, :], ps_q[:, :].rearrange("p (a t) -> p a t", a=2),
                               ACT.Copy, scale=-HD ** -0.5).then_inc(q_hi, 1)

            def v_copy(s, i):
                wait(act, v_ready, 4 * s + i + 1)
                act.activation(v_sb[:, i % 2, 512 * (i // 2):512 * (i // 2) + 512], ps_v[:, :], ACT.Copy)\
                   .then_inc(v_copied, 1)

            def exps(n, u, sign):
                wait(act, max_ready, n + 1)
                wait(act, pt_ready, n - 3)
                for h in range(4):
                    last = act.activation(probs[:, u % 4, h, :], ps_s[u % 2][:, h * T:(h + 1) * T], ACT.Exp,
                                          scale=sign, bias=nmax[:, u % 4, h:h + 1], accum_out=den[:, u % 4, h:h + 1])
                last.then_inc(exp_done, 1)

            def o_copy(n, u, narrow):
                wait(act, o_ready, n + 1)
                jj, b = u // 2, u % 2
                if narrow is None:
                    act.activation(oT[:, 2 * jj:2 * jj + 2, b * T:(b + 1) * T],
                                   ps_o[:, 0:2 * T].rearrange("p (a t) -> p a t", a=2), ACT.Copy)\
                       .then_inc(o_copied, 1)
                else:
                    act.activation(noT[narrow][:, jj, b * T:(b + 1) * T], ps_o[:, 0:T], ACT.Copy)\
                       .then_inc(o_copied, 1)

            def upper(s, pieces, follow):
                for what, i, ahead in pieces:
                    if ahead and not follow:
                        continue
                    if what == "k":
                        k_upper(s + ahead, i)
                    elif what == "q":
                        q_upper(s + ahead, i)
                    elif what == "v":
                        v_copy(s, i)

            def wide_step(t, s, g, layer, head=False, follow=True, fresh=False):
                gn = 0 if fresh else g + 1
                for u in range(SLOTS):
                    n = 8 * t + u
                    if u:
                        upper(s, PIECES[u - 1], follow)
                    elif not head:
                        upper(s - 1, PIECES[7], True)
                    if fresh:
                        for c in REFRESH.get(u, ()):
                            split(c, layer + 1)
                    if u == 4 and follow:
                        split_x(s + 1, gn, 0 if layer == 0 and not fresh else 2 * (t - 6))
                    exps(n, u, -1.0)
                    if not (head and u < PLAG):
                        o_copy(n - PLAG, (u - PLAG) % 8, None)

            def flush(t, narrow):
                for m in range(PLAG, 0, -1):
                    o_copy(8 * t - m, 8 - m, narrow)

            def first_pieces(s):
                for what, i in FIRST_PIECES:
                    (k_upper if what == "k" else q_upper)(s, i)

            act.wait_ge(setup_hi, 12)
            for c in range(6):
                split(c, 0)
                if c == 0:
                    split_x(0, 0, 0)
            first_pieces(0)
            wide_step(0, 0, 0, 0, head=True)
            with act.Fori(1, G - 1) as s:
                wide_step(s, s, s, 0)
            wide_step(G - 1, G - 1, G - 1, 0, fresh=True)
            wide_step(G, G, 0, 1)
            with act.Fori(G + 1, 2 * G - 1) as s:
                wide_step(s, s, s - G, 1)
            wide_step(2 * G - 1, 2 * G - 1, G - 1, 1, follow=False)
            flush(2 * G, None)

            for i in range(4):
                act.wait_ge(mean_ready, i + 1)
                act.activation(probs[:, i, :, :].rearrange("p h t -> p (h t)"),
                               [ps_s[0], ps_s[1], ps_q, ps_v][i][:, :], ACT.Sqrt, bias=eps_sb[:, :])\
                   .then_inc(root_ready, 1)
            for i in range(4):
                act.wait_ge(xn_ready, i + 1)
                act.activation(k_hf[:, XN0 + 512 * i:XN0 + 512 * i + 512],
                               probs[:, i, :, :].rearrange("p h t -> p (h t)"), ACT.Copy).then_inc(xn_hi, 1)

            def nk_upper(g, e):
                wait(act, nk_ready, g + 1)
                for h in range(KV):
                    rows = slice(32 * h, 32 * h + 32)
                    last = act.activation(nk_h[e][rows, h, :], ps_k[1][rows, 0:GT], ACT.Copy)
                last.then_inc(nk_hi, 1)

            def nq_upper(g, e, half):
                wait(act, nq_ready, 2 * g + half + 1)
                act.activation(nq_h[e][:, 2 * half:2 * half + 2, :],
                               ps_q[:, :].rearrange("p (a t) -> p a t", a=2), ACT.Copy,
                               scale=RD ** -0.5).then_inc(nq_hi, 1)

            def nv_copy(g, e):
                wait(act, nv_ready, g + 1)
                act.activation(nv[e], ps_v[:, 0:GB * P].rearrange("p (b n) -> p b n", b=GB), ACT.Copy)\
                   .then_inc(nv_copied, 1)

            def narrow_step(t, g, e, head=False, follow=True):
                for u in range(SLOTS):
                    if u and follow:
                        for what, i, _ in NPIECES.get(u - 1, ()):
                            if what == "k":
                                nk_upper(g + 1, 1 - e)
                            elif what == "q":
                                nq_upper(g + 1, 1 - e, i)
                    elif not u and not head:
                        nv_copy(g, e)
                    exps(8 * t + u, u, 1.0)
                    if not (head and u < PLAG):
                        o_copy(8 * t + u - PLAG, (u - PLAG) % 8, e if u >= PLAG else 1 - e)

            act.wait_ge(k_cleared, 6)
            nk_upper(0, 0)
            nq_upper(0, 0, 0)
            nq_upper(0, 0, 1)
            nv_copy(0, 0)
            narrow_step(NARROW_AT, 0, 0, head=True)
            narrow_step(NARROW_AT + 1, 1, 1)
            with act.Fori(1, G // 2 - 1) as i:
                for e in range(2):
                    narrow_step(2 * i + (NARROW_AT + e), 2 * i + e, e)
            narrow_step(LAST_AT - 2, G - 2, 0)
            narrow_step(LAST_AT - 1, G - 1, 1, follow=False)
            flush(LAST_AT, 1)

            for c in range(6):
                split(c, 2)
            split_x(2 * G, 0, 2 * LAST_AT)
            act.wait_ge(k_cleared, 10)
            first_pieces(2 * G)
            wide_step(LAST_AT, 2 * G, 0, 2, head=True)
            with act.Fori(1, G - 1) as g:
                wide_step(g + LAST_AT, g + 2 * G, g, 2)
            wide_step(4 * G - 1, 3 * G - 1, G - 1, 2, follow=False)
            flush(4 * G, None)

        @block.vector
        def _(dve):
            done = [0]

            def then(ins):
                done[0] += 1
                ins.then_inc(rows_step, 1)
                dve.wait_ge(rows_step, done[0])

            then(dve.memset(alpha[:, :].bitcast(F32), 0.0))
            then(dve.memset(sel[:, :, :].bitcast(F32), 0.0))
            then(dve.memset(flag[:, :], 0.0))
            then(dve.memset(flag[0:1, :], 1.0))
            then(dve.memset(flag[32:33, :], 1.0))
            then(dve.memset(eps_sb[:, :], EPS))
            dve.wait_ge(small_loaded, 16 * 8)
            then(dve.tensor_scalar(mrow[:, :], mrow[:, :], -1.0, 1.0, ALU.mult, ALU.add))
            then(dve.tensor_scalar(mrow[:, :], mrow[:, :], SUPPRESS, None, ALU.mult))
            then(dve.tensor_copy(mhi[:, :], mrow[:, :]))
            then(dve.tensor_copy(alpha[0:2, :], mrow[0:2, :]))
            then(dve.tensor_tensor(alpha[32:34, :], mrow[32:34, :], mhi[32:34, :].bitcast(F32), ALU.subtract))
            dve.wait_ge(ident_ready, 2)
            then(dve.tensor_copy(iota_f[:, :], iota_i[:, :]))
            src = idx_i[:, :, :].rearrange("p l (k c) -> p l k c", k=2)
            then(dve.tensor_copy(idx_f[:, :, :, 0:2], src))
            then(dve.tensor_scalar(idx_f[:, :, :, 2:4], idx_f[:, :, :, 0:2], float(T), None, ALU.add))
            for layer in range(WIDE):
                for k in range(2):
                    hit = ps_o[0:64, :].rearrange("p (j t) -> p j t", j=4)
                    then(dve.tensor_tensor(hit, iota_f[:, :].unsqueeze(1).to_broadcast([64, 4, T]),
                                           idx_f[:, layer, k, :].unsqueeze(2).to_broadcast([64, 4, T]),
                                           ALU.is_equal))
                    then(dve.tensor_reduce(picked[:, k, :], hit.rearrange("p j t -> p t j"), AX.X, ALU.max))
                then(dve.scalar_tensor_tensor(out=both[:, :], in0=picked[:, 1, :], scalar=flag[:, 0:1],
                                              in1=picked[:, 0, :], op0=ALU.mult, op1=ALU.mult))
                then(dve.tensor_tensor(sel[0:64, layer, :], picked[:, 0, :], both[:, :], ALU.subtract))
            dve.memset(flag[:, :], 0.0).then_inc(rows_ready, 1)

            for i in range(8):
                dve.wait_ge(setup_hi, i + 1)
                cols = slice(512 * (i // 2), 512 * (i // 2) + 512)
                dve.tensor_tensor(c_l[:, i % 2, cols], setup_banks[i % 6][:, :],
                                  c_h[:, i % 2, cols].bitcast(F32), ALU.subtract).then_inc(setup_lo, 1)

            def split(c, layer):
                dve.wait_ge(w_hi, 6 * layer + c + 1)
                dve.tensor_tensor(chunk(w_l, c), chunk(w_raw, c), chunk(w_h, c).bitcast(F32), ALU.subtract)\
                   .then_inc(w_lo, 1)

            def split_x(s, g):
                wait(dve, xs_hi, s + 1)
                dve.tensor_tensor(xs_l[:, :], xT[:, step_cols(g)], xs_h[:, :].bitcast(F32), ALU.subtract)\
                   .then_inc(xs_lo, 1)

            def k_lower(s, jj):
                wait(dve, k_hi, 4 * s + jj + 1)
                src = ps_k[K_BANK["k", jj]][:, :].rearrange("p (a t) -> p a t", a=2)
                for half in range(2):
                    rows = slice(64 * half, 64 * half + 64)
                    pair = slice(2 * jj, 2 * jj + 2)
                    last = dve.tensor_tensor(k_l[rows, pair, half, :], src[rows],
                                             k_h[rows, pair, half, :].bitcast(F32), ALU.subtract)
                last.then_inc(k_lo, 1)

            def q_lower(s, jj):
                wait(dve, q_hi, 4 * s + jj + 1)
                pair = slice(2 * jj, 2 * jj + 2)
                dve.scalar_tensor_tensor(out=q_l[:, pair, :], in0=ps_q[:, :].rearrange("p (a t) -> p a t", a=2),
                                         scalar=-HD ** -0.5, in1=q_h[:, pair, :].bitcast(F32), op0=ALU.mult,
                                         op1=ALU.subtract).then_inc(q_lo, 1)

            def update_x(t, g, b, layer):
                wait(dve, y_ready, 2 * t - 1 + b)
                xg = xT[:, bass.ds(g * GT + b * T, T)]
                src = ps_k[K_BANK["y", b]][:, 0:T]
                if layer is None:
                    dve.tensor_tensor(xg, src, xg, ALU.add).then_inc(x_updated, 1)
                else:
                    dve.scalar_tensor_tensor(out=xg, in0=src, scalar=bo_sb[:, layer:layer + 1], in1=xg,
                                             op0=ALU.add, op1=ALU.add).then_inc(x_updated, 1)

            def maxima(n, u):
                wait(dve, scores_ready, n + 1)
                dve.tensor_reduce(nmax[:, u % 4, :], ps_s[u % 2][:, :].rearrange("p (h t) -> p h t", h=4),
                                  AX.X, ALU.max, negate=True).then_inc(max_ready, 1)

            def minima(n, u, layer):
                wait(dve, scores_ready, n + 1)
                dve.memset(gate[:, :], 0.0)
                for h in range(4):
                    sc = ps_s[u % 2][:, h * T:(h + 1) * T]
                    last = dve.tensor_tensor_reduce(sc, sc, bias[:, layer, :], 1.0, FAR, ALU.add, ALU.min,
                                                    nmax[:, u % 4, h:h + 1])
                last.then_inc(max_ready, 1)

            def sums(n, u):
                wait(dve, exp_done, n + 1)
                dve.reciprocal(rden[:, u % 4, :], den[:, u % 4, :]).then_inc(rden_ready, 1)

            def pt_copy(n, u):
                wait(dve, pt_ready, n + 1)
                wait(dve, o_ready, n - 1)
                dve.tensor_copy(probsT[:, u % 2, :, :], ps_t[:, :].rearrange("p (h t) -> p h t", h=4))\
                   .then_inc(pt_copied, 1)

            def lower(s, pieces, follow):
                for what, i, ahead in pieces:
                    if ahead and not follow:
                        continue
                    if what == "k":
                        k_lower(s + ahead, i)
                    elif what == "q":
                        q_lower(s + ahead, i)

            def wide_step(t, s, g, layer, head=False, follow=True, fresh=False):
                gn = 0 if fresh else g + 1
                start = isinstance(s, int) and s % G == 0
                for u in range(SLOTS):
                    n = 8 * t + u
                    if not (head and u < 1):
                        sums(n - 1, (u - 1) % 8)
                    minima(n, u, layer)
                    if not (head and u < TLAG):
                        pt_copy(n - TLAG, (u - TLAG) % 8)
                    if u - 1 in Y_AT and not head:
                        update_x(t, G - 1 if start else g - 1, Y_AT.index(u - 1),
                                 layer - 1 if start else layer)
                    if u:
                        lower(s, PIECES[u - 1], follow)
                    elif not head:
                        lower(s - 1, PIECES[7], True)
                    if fresh:
                        for c in REFRESH.get(u, ()):
                            split(c, layer + 1)
                    if u == 4 and follow:
                        split_x(s + 1, gn)

            def flush(t, g, layer):
                sums(8 * t - 1, 7)
                for m in (2, 1):
                    pt_copy(8 * t - m, 8 - m)
                for b in range(GB):
                    update_x(t, g, b, layer)

            def first_pieces(s):
                for what, i in FIRST_PIECES:
                    (k_lower if what == "k" else q_lower)(s, i)

            dve.wait_ge(bias_made, 1)
            dve.tensor_copy(bias[:, :, :].rearrange("p l t -> p (l t)"), ps_t[:, 0:WIDE * T])\
               .then_inc(bias_ready, 1)
            for c in range(6):
                split(c, 0)
                if c == 0:
                    split_x(0, 0)
            dve.wait_ge(columns_loaded, 16 * 2)
            first_pieces(0)
            dve.wait_ge(narrow_loaded, 16 * (REP * 5 + 4))
            dve.tensor_copy(nw_h[:, :, :], nw_raw).then_inc(nw_hi, 1)
            dve.wait_ge(nw_hi, 1)
            dve.tensor_tensor(nw_l[:, :, :], nw_raw, nw_h[:, :, :].bitcast(F32), ALU.subtract).then_inc(nw_lo, 1)
            wide_step(0, 0, 0, 0, head=True)
            with dve.Fori(1, G - 1) as s:
                wide_step(s, s, s, 0)
            wide_step(G - 1, G - 1, G - 1, 0, fresh=True)
            wide_step(G, G, 0, 1)
            with dve.Fori(G + 1, 2 * G - 1) as s:
                wide_step(s, s, s - G, 1)
            wide_step(2 * G - 1, 2 * G - 1, G - 1, 1, follow=False)
            flush(2 * G, G - 1, 1)

            dve.wait_ge(x_updated, 2 * NARROW_AT)
            for i in range(4):
                xi = xT[:, 512 * i:512 * i + 512]
                dve.tensor_tensor(probs[:, i, :, :].rearrange("p h t -> p (h t)"), xi, xi, ALU.mult)\
                   .then_inc(sq_ready, 1)
            for i in range(4):
                pi = probs[:, i, :, :].rearrange("p h t -> p (h t)")
                dve.wait_ge(root_ready, i + 1)
                dve.reciprocal(pi, pi).then_inc(inv_ready, 1)
                dve.wait_ge(inv_ready, i + 1)
                dve.scalar_tensor_tensor(out=pi, in0=xT[:, 512 * i:512 * i + 512], scalar=nw_sb[:, 0:1], in1=pi,
                                         op0=ALU.mult, op1=ALU.mult).then_inc(xn_ready, 1)
            for i in range(4):
                dve.wait_ge(xn_hi, i + 1)
                cols = slice(XN0 + 512 * i, XN0 + 512 * i + 512)
                dve.tensor_tensor(k_lf[:, cols], probs[:, i, :, :].rearrange("p h t -> p (h t)"),
                                  k_hf[:, cols].bitcast(F32), ALU.subtract).then_inc(xn_lo, 1)

            def nk_lower(g, e):
                wait(dve, nk_hi, g + 1)
                for h in range(KV):
                    rows = slice(32 * h, 32 * h + 32)
                    last = dve.tensor_tensor(nk_l[e][rows, h, :], ps_k[1][rows, 0:GT],
                                             nk_h[e][rows, h, :].bitcast(F32), ALU.subtract)
                last.then_inc(nk_lo, 1)

            def nq_lower(g, e, half):
                wait(dve, nq_hi, 2 * g + half + 1)
                r = slice(2 * half, 2 * half + 2)
                dve.scalar_tensor_tensor(out=nq_l[e][:, r, :], in0=ps_q[:, :].rearrange("p (a t) -> p a t", a=2),
                                         scalar=RD ** -0.5, in1=nq_h[e][:, r, :].bitcast(F32), op0=ALU.mult,
                                         op1=ALU.subtract).then_inc(nq_lo, 1)

            def narrow_step(t, g, e, head=False, follow=True):
                for u in range(SLOTS):
                    n = 8 * t + u
                    if not (head and u < 1):
                        sums(n - 1, (u - 1) % 8)
                    maxima(n, u)
                    if not (head and u < TLAG):
                        pt_copy(n - TLAG, (u - TLAG) % 8)
                    if u - 1 in Y_AT and not head:
                        update_x(t, g - 1, Y_AT.index(u - 1), None)
                    if u and follow:
                        for what, i, _ in NPIECES.get(u - 1, ()):
                            if what == "k":
                                nk_lower(g + 1, 1 - e)
                            elif what == "q":
                                nq_lower(g + 1, 1 - e, i)

            nk_lower(0, 0)
            nq_lower(0, 0, 0)
            nq_lower(0, 0, 1)
            narrow_step(NARROW_AT, 0, 0, head=True)
            narrow_step(NARROW_AT + 1, 1, 1)
            with dve.Fori(1, G // 2 - 1) as i:
                for e in range(2):
                    narrow_step(2 * i + (NARROW_AT + e), 2 * i + e, e)
            narrow_step(LAST_AT - 2, G - 2, 0)
            narrow_step(LAST_AT - 1, G - 1, 1, follow=False)
            flush(LAST_AT, G - 1, None)

            for c in range(6):
                split(c, 2)
            split_x(2 * G, 0)
            first_pieces(2 * G)
            wide_step(LAST_AT, 2 * G, 0, 2, head=True)
            with dve.Fori(1, G - 1) as g:
                wide_step(g + LAST_AT, g + 2 * G, g, 2)
            wide_step(4 * G - 1, 3 * G - 1, G - 1, 2, follow=False)
            flush(4 * G, G - 1, 2)

            for q in range(4):
                dve.wait_ge(fin_t, q + 1)
                dve.tensor_copy(probs[:, q, :, :].rearrange("p h t -> p (h t)"),
                                [ps_s[0], ps_s[1], ps_q, ps_v][q][:, :]).then_inc(fin_copied, 1)


def kernel(**inputs):
    import numpy as _np
    import concourse.bacc as _bacc
    from concourse import mybir as _mybir
    from concourse.bass_utils import run_bass_kernel_spmd as _run

    a = {k: _np.asarray(v) for k, v in inputs.items()}
    wide = ("L0", "L1", "L3")

    def stacked(name):
        return _np.stack([a[f"{w}_xattn_{name}"] for w in wide])

    arrays = {
        "x": a["x"], "ctx_in": a["ctx_2048"], "masks": _np.stack([a["mask_S_fk1"], a["mask_S_fk0"]]),
        "tokens": _np.stack([stacked("token_indices_A"), stacked("token_indices_B")], axis=1),
        "wq": stacked("Wq"), "wk": stacked("Wk"), "wv": stacked("Wv"), "wo": stacked("Wo"), "bo": stacked("bo").T,
        "nwq": a["L2_xattn_wq"], "nwk": a["L2_xattn_wk"], "nwv": a["L2_xattn_wv"], "nwo": a["L2_xattn_wo"],
        "nw": a["L2_xattn_norm_w"][:, None],
    }
    arrays = {f"in_{k}": _np.ascontiguousarray(v) for k, v in arrays.items()}
    nc = _bacc.Bacc("TRN2", target_bir_lowering=False, num_devices=1)
    args = [nc.dram_tensor(k, v.shape, _mybir.dt.from_np(v.dtype), kind="ExternalInput").ap()
            for k, v in arrays.items()]
    args.append(nc.dram_tensor("out_x", (B, T, C), _mybir.dt.float32, kind="ExternalOutput").ap())
    build_program(nc, *args)
    r = _run(nc, [arrays], core_ids=[0])
    return r.results[0]["out_x"]
```

```python
from contextlib import ExitStack

import concourse.bass as bass
from concourse import mybir

F32 = mybir.dt.float32
F32R = mybir.dt.float32r
ALU = mybir.AluOpType
ACT = mybir.ActivationFunctionType
AX = mybir.AxisListType

P = 128
B, T, C = 16, 128, 128
CT, KT = 256, 2
HEADS, HD = 16, 64
INNER = HEADS * HD
PAIRS = HEADS // 2
KV, RD = 4, 8
REP = HEADS // KV
GB = 2
G = B // GB
GT = GB * T
SLOTS = 8
SUPPRESS = 20.0
EPS = 1e-5
FAR = 3.4e38
CHUNK = 3 * 256
WV0 = 4 * CHUNK
WCOLS = WV0 + KT * INNER
WIDE = 3
NARROW_AT = 2 * G
LAST_AT = 3 * G


def build_program(nc, x, ctx_in, masks, tokens, wq, wk, wv, wo, bo, nwq, nwk, nwv, nwo, nw, out):
    with ExitStack() as stack:
        def sb(name, shape, dt=F32):
            return stack.enter_context(nc.sbuf_tensor(name, shape, dt))

        def sem(name):
            return stack.enter_context(nc.semaphore(name))

        xT = sb("xT", [P, B * T])
        xs_h, xs_l = sb("xs_h", [P, GT], F32R), sb("xs_l", [P, GT], F32R)
        c_h, c_l = sb("c_h", [P, KT, B * T], F32R), sb("c_l", [P, KT, B * T], F32R)
        cv_h, cv_l = sb("cv_h", [P, GB, KT, T], F32R), sb("cv_l", [P, GB, KT, T], F32R)
        w_h, w_l = sb("w_h", [P, WCOLS], F32R), sb("w_l", [P, WCOLS], F32R)
        w_raw = sb("w_raw", [P, 2, KT * INNER // 2])
        wo_raw = sb("wo_raw", [P, 2, 2, C])
        wo_h, wo_l = sb("wo_h", [P, PAIRS, C], F32R), sb("wo_l", [P, PAIRS, C], F32R)
        k_h, k_l = sb("k_h", [P, PAIRS, 2, GT], F32R), sb("k_l", [P, PAIRS, 2, GT], F32R)
        q_h, q_l = sb("q_h", [P, PAIRS, GT], F32R), sb("q_l", [P, PAIRS, GT], F32R)
        v_sb = sb("v_sb", [P, GB, INNER])
        o_h, o_l = sb("o_h", [P, 2, 2, GT], F32R), sb("o_l", [P, 2, 2, GT], F32R)
        probs = sb("probs", [P, 4, 4, T])
        probsT = sb("probsT", [P, 2, 4, T])
        nmax = sb("nmax", [P, 4, 4])
        den = sb("den", [P, 4, 4])
        rden = sb("rden", [P, 4, 4])
        ident = sb("ident", [P, P])
        mean_w = sb("mean_w", [P, 1])
        alpha = sb("alpha", [P, T], F32R)
        sel = sb("sel", [P, WIDE, T], F32R)
        bias = sb("bias", [P, WIDE, T])
        bo_sb = sb("bo_sb", [P, WIDE])
        nw_sb = sb("nw_sb", [P, 1])
        eps_sb = sb("eps_sb", [P, 1])
        nw_h, nw_l = sb("nw_h", [P, 8, P], F32R), sb("nw_l", [P, 8, P], F32R)
        nwo_h, nwo_l = sb("nwo_h", [P, REP, C], F32R), sb("nwo_l", [P, REP, C], F32R)
        sq = sb("sq", [P, B * T])
        last_x = sb("last_x", [P, GT])
        result_sb = sq
        root = sb("root", [P, B])
        inv = sb("inv", [P, 2, GB])
        peak = sb("peak", [P, 4, 4])
        gate = sb("gate", [P, 1])
        mrow = sb("mrow", [64, T])
        mhi = sb("mhi", [64, T], F32R)
        idx_i = sb("idx_i", [64, WIDE, 4], mybir.dt.int32)
        idx_f = sb("idx_f", [64, WIDE, 2, 4])
        flag = sb("flag", [64, 1])
        iota_i = sb("iota_i", [64, T], mybir.dt.int32)
        iota_f = sb("iota_f", [64, T])

        x_raw = sq[:, :]
        picked = last_x[0:64, :].rearrange("p (k t) -> p k t", k=2)
        both = probsT[0:64, 1, 3, :]
        nw_raw = sq[:, 0:8 * P].rearrange("p (m n) -> p m n", m=8)
        nwo_raw = sq[:, 8 * P:8 * P + REP * C].rearrange("p (r n) -> p r n", r=REP)
        ctx_raw = [v_sb[:].rearrange("p b n -> p (b n)"), probs[:].rearrange("p r h t -> p (r h t)")]
        k_hf, k_lf = (k[:].rearrange("p a s t -> p (a s t)") for k in (k_h, k_l))
        q_hf, q_lf = (q[:].rearrange("p a t -> p (a t)") for q in (q_h, q_l))
        NK = KV * GT
        NK_AT = [0, 2 * GT * PAIRS - NK]
        nk_h, nk_l = ([k[:, at:at + NK].rearrange("p (g t) -> p g t", g=KV) for at in NK_AT]
                      for k in (k_hf, k_lf))
        nq_h, nq_l = ([q[:, e * REP * GT:(e + 1) * REP * GT].rearrange("p (r t) -> p r t", r=REP)
                       for e in range(2)] for q in (q_hf, q_lf))
        nv = [v_sb[:, e, 0:GB * P].rearrange("p (b n) -> p b n", b=GB) for e in range(2)]

        def bank(name):
            return stack.enter_context(nc.psum_tensor(name, [P, 512], F32))

        ps_s = [bank("ps_s0"), bank("ps_s1")]
        ps_t = bank("ps_t")
        ps_o = bank("ps_o")
        ps_k = bank("ps_k")
        ps_q = bank("ps_q")
        ps_v = bank("ps_v")
        ps_y = bank("ps_y")
        setup_banks = [ps_s[0], ps_s[1], ps_k, ps_y, ps_q, ps_v]

        scores_ready = sem("scores_ready")
        max_ready = sem("max_ready")
        exp_done = sem("exp_done")
        rden_ready = sem("rden_ready")
        norm_done = sem("norm_done")
        pt_ready = sem("pt_ready")
        pt_copied = sem("pt_copied")
        o_ready = sem("o_ready")
        o_hi, o_lo = sem("o_hi"), sem("o_lo")
        k_ready, k_hi, k_lo = sem("k_ready"), sem("k_hi"), sem("k_lo")
        q_ready, q_hi, q_lo = sem("q_ready"), sem("q_hi"), sem("q_lo")
        v_ready, v_copied = sem("v_ready"), sem("v_copied")
        nk_ready, nk_hi, nk_lo = sem("nk_ready"), sem("nk_hi"), sem("nk_lo")
        nq_ready, nq_hi, nq_lo = sem("nq_ready"), sem("nq_hi"), sem("nq_lo")
        nv_ready, nv_copied = sem("nv_ready"), sem("nv_copied")
        y_ready, x_updated = sem("y_ready"), sem("x_updated")
        xs_hi, xs_lo = sem("xs_hi"), sem("xs_lo")
        cv_loaded = [sem("cv_loaded0"), sem("cv_loaded1")]
        w_loaded = [sem(f"w_loaded{c}") for c in range(6)]
        w_hi, w_lo = sem("w_hi"), sem("w_lo")
        wo_loaded = [sem(f"wo_loaded{part}") for part in range(4)]
        wo_hi, wo_lo = sem("wo_hi"), sem("wo_lo")
        x_loaded = sem("x_loaded")
        ctx_loaded = [sem("ctx_loaded0"), sem("ctx_loaded1")]
        small_loaded, columns_loaded = sem("small_loaded"), sem("columns_loaded")
        narrow_loaded = sem("narrow_loaded")
        zeroed = sem("zeroed")
        ident_ready = sem("ident_ready")
        setup_t, setup_hi, setup_lo = sem("setup_t"), sem("setup_hi"), sem("setup_lo")
        rows_step, rows_ready, bias_made, bias_ready = (sem("rows_step"), sem("rows_ready"), sem("bias_made"),
                                                        sem("bias_ready"))
        nw_hi, nw_lo = sem("nw_hi"), sem("nw_lo")
        k_cleared = sem("k_cleared")
        sq_ready, mean_ready, root_ready = sem("sq_ready"), sem("mean_ready"), sem("root_ready")
        inv_ready, peak_ready = sem("inv_ready"), sem("peak_ready")
        fin_t, fin_copied, stored = sem("fin_t"), sem("fin_copied"), sem("stored")

        def wait(eng, semaphore, value):
            if not isinstance(value, int) or value > 0:
                eng.wait_ge(semaphore, value)

        PIECES = {"wide": {0: [("k", 2, 0)], 1: [("v", 0, 0), ("q", 2, 0)], 2: [("k", 3, 0)],
                           3: [("v", 1, 0), ("q", 3, 0)], 4: [("k", 0, 1)], 5: [("v", 2, 0), ("q", 0, 1)],
                           6: [("k", 1, 1)], 7: [("q", 1, 1), ("v", 3, 0)]},
                  "narrow": {2: [("nv", 0, 0)], 4: [("nk", 0, 1)], 5: [("nq", 0, 1)], 7: [("nq", 1, 1)]}}
        FIRST_PIECES = [("k", 0), ("q", 0), ("k", 1), ("q", 1)]
        TLAG, PLAG, OLAG = 2, 3, 4
        XS_AT = 4
        UPDATE_AT = 5
        REFRESH = {0: 0, 3: 1, 5: 2, 6: 3, 7: 4}
        REFRESH_5 = 3
        REFRESH_WO = {1: 0, 3: 1, 5: 2, 7: 3}
        EARLY = 2 * (G - 2)
        MEAN_AT = 6

        def pieces(u, cur, nxt):
            found = []
            for kind, mine, ahead in (("wide", cur == "wide", nxt == "wide"),
                                      ("narrow", cur == "narrow", nxt == "narrow")):
                found += [p for p in PIECES[kind].get(u, ()) if (ahead if p[2] else mine)]
            return found

        def chunk(t, c):
            if c < 4:
                return t[:, c * CHUNK:(c + 1) * CHUNK]
            n = KT * INNER // 2
            return t[:, WV0 + (c - 4) * n:WV0 + (c - 3) * n]

        def raw(layer, c):
            if layer == 0 and c == 2:
                return probsT[:, :, :, :].rearrange("p r h t -> p (r h t)")[:, 0:CHUNK]
            turn = (c + (c > 2)) % 2 if layer == 0 else c % 2
            return w_raw[:, turn, 0:CHUNK if c < 4 else KT * INNER // 2]

        def raw_free(layer, c):
            if layer == 0:
                return {3: 1, 4: 2, 5: 4}.get(c, 0)
            return 6 * layer + max(c - 1, 0)

        def step_cols(g):
            return bass.ds(g * GT, GT)

        def walk(eng, step):
            w, n = "wide", "narrow"
            step(0, 0, 0, 0, None, w, w)
            with eng.Fori(1, G - 2) as s:
                step(s, s, s, 0, w, w, w)
            step(G - 2, G - 2, G - 2, 0, w, w, w)
            step(G - 1, G - 1, G - 1, 0, w, w, w)
            step(G, G, 0, 1, w, w, w)
            with eng.Fori(G + 1, 2 * G - 1) as s:
                step(s, s, s - G, 1, w, w, w)
            step(2 * G - 1, 2 * G - 1, G - 1, 1, w, w, n)
            step(NARROW_AT, 2 * G, 0, None, w, n, n)
            step(NARROW_AT + 1, 2 * G, 1, None, n, n, n)
            with eng.Fori(1, G // 2 - 1) as i:
                for e in range(2):
                    step(2 * i + (NARROW_AT + e), 2 * G, 2 * i + e, None, n, n, n, e)
            step(LAST_AT - 2, 2 * G, G - 2, None, n, n, n)
            step(LAST_AT - 1, 2 * G, G - 1, None, n, n, w)
            step(LAST_AT, 2 * G, 0, 2, n, w, w)
            with eng.Fori(1, G - 1) as g:
                step(g + LAST_AT, g + 2 * G, g, 2, w, w, w)
            step(4 * G - 1, 3 * G - 1, G - 1, 2, w, w, None)

        block = stack.enter_context(nc.Block())

        @block.sync
        def _(sp):
            def load_chunk(layer, c):
                wait(sp, w_hi, raw_free(layer, c))
                wait(sp, w_lo, raw_free(layer, c))
                dst = raw(layer, c)
                if c < 4:
                    cols = slice(256 * c, 256 * c + 256)
                    dst = dst.rearrange("p (m n) -> p m n", m=3)
                    sp.dma_start(dst[:, 0:KT, :],
                                 wk[layer].rearrange("(k p) n -> p k n", p=P)[:, :, cols]).then_inc(w_loaded[c], 16)
                    sp.dma_start(dst[:, KT, :], wq[layer, :, cols]).then_inc(w_loaded[c], 16)
                else:
                    sp.dma_start(dst.rearrange("p (k n) -> p k n", k=KT),
                                 wv[layer].rearrange("(k p) n -> p k n", p=P)[:, :, 512 * (c - 4):512 * (c - 3)])\
                      .then_inc(w_loaded[c], 16)

            def load_wo(layer, part):
                wait(sp, wo_hi, 4 * layer + part - 1)
                wait(sp, wo_lo, 4 * layer + part - 1)
                sp.dma_start(wo_raw[:, part % 2, :, :],
                             wo[layer, 256 * part:256 * part + 256].rearrange("(a p) n -> p a n", p=P))\
                  .then_inc(wo_loaded[part], 16)

            def load_cv(g, b, after):
                if after is not None:
                    wait(sp, after[0], after[1])
                for dst, src in ((cv_h, c_h), (cv_l, c_l)):
                    sp.dma_start(dst[:, b, :, :].bitcast(F32), src[:, :, bass.ds(g * GT + b * T, T)].bitcast(F32))\
                      .then_inc(cv_loaded[b], 16)

            def refresh(layer):
                s = G * layer + G - 1
                sp.wait_ge(q_ready, 4 * s + 1)
                sp.wait_ge(k_ready, 4 * s + 1)
                load_chunk(layer + 1, 0)
                for b in range(GB):
                    load_cv(G - 1, b, (v_ready, 4 * s - 1 + b))
                sp.wait_ge(q_ready, 4 * s + 2)
                sp.wait_ge(k_ready, 4 * s + 2)
                load_chunk(layer + 1, 1)
                sp.wait_ge(q_ready, 4 * s + 3)
                sp.wait_ge(k_ready, 4 * s + 3)
                load_chunk(layer + 1, 2)
                sp.wait_ge(q_ready, 4 * s + 4)
                sp.wait_ge(k_ready, 4 * s + 4)
                load_chunk(layer + 1, 3)
                sp.wait_ge(v_ready, 4 * s + 2)
                load_chunk(layer + 1, 4)
                load_cv(0, 0, (v_ready, 4 * s + 3))
                sp.wait_ge(y_ready, 4 * s + 1)
                load_wo(layer + 1, 0)
                load_cv(0, 1, (v_ready, 4 * s + 4))
                load_chunk(layer + 1, 5)
                for part in range(1, 4):
                    sp.wait_ge(y_ready, 4 * s + part + 1)
                    load_wo(layer + 1, part)

            for h in range(2):
                sp.dma_start(ctx_raw[h].rearrange("p (b c) -> p b c", c=CT),
                             ctx_in[8 * h:8 * h + 8].rearrange("b t c -> t b c")).then_inc(ctx_loaded[h], 16)
            sp.wait_ge(zeroed, 2)
            for base in (0, 32):
                sp.dma_start(mrow[base:base + 2, :], masks).then_inc(small_loaded, 16)
                sp.dma_start(idx_i[base:base + 2, :, 0:2], tokens.rearrange("l r c -> r l c"))\
                  .then_inc(small_loaded, 16)
                for r in range(2):
                    sp.dma_start(idx_i[base + r:base + r + 1, :, 2:4],
                                 tokens[:, 1:2, :].rearrange("l r c -> r l c")).then_inc(small_loaded, 16)
            for c in range(5):
                load_chunk(0, c)
            for part in range(2):
                load_wo(0, part)
            sp.dma_start(bo_sb[:, :], bo).then_inc(columns_loaded, 16)
            sp.dma_start(nw_sb[:, :], nw).then_inc(columns_loaded, 16)
            sp.wait_ge(setup_hi, 12)
            sp.wait_ge(setup_lo, 8)
            for b in range(GB):
                load_cv(0, b, None)
            sp.wait_ge(zeroed, 4)
            for r in range(REP):
                sp.dma_start(nw_raw[:, r, :].rearrange("p (g d) -> p g d", g=KV)[:, :, 0:RD],
                             nwq.rearrange("p (g r d) -> p g r d", g=KV, r=REP)[:, :, r, :])\
                  .then_inc(narrow_loaded, 16)
                for g in range(KV):
                    h = g * REP + r
                    sp.dma_start(nwo_raw[32 * g:32 * g + RD, r, :], nwo[h * RD:(h + 1) * RD, :])\
                      .then_inc(narrow_loaded, 16)
            for i, w in enumerate((nwk, nwv)):
                for k in range(KT):
                    sp.dma_start(nw_raw[:, 4 + 2 * i + k, :].rearrange("p (g d) -> p g d", g=KV)
                                 [:, :, 0:RD], w[k * P:(k + 1) * P, :].rearrange("p (g d) -> p g d", g=KV))\
                      .then_inc(narrow_loaded, 16)

            load_chunk(0, 5)
            for part in range(2, 4):
                load_wo(0, part)

            with sp.Fori(1, G - 1) as s:
                for b in range(GB):
                    load_cv(s, b, (v_ready, 4 * s - 1 + b))
            refresh(0)
            with sp.Fori(G + 1, 2 * G - 1) as s:
                for b in range(GB):
                    load_cv(s - G, b, (v_ready, 4 * s - 1 + b))
            refresh(1)
            with sp.Fori(1, G) as g:
                for b in range(GB):
                    load_cv(g, b, (nv_ready, g))
            for b in range(GB):
                load_cv(0, b, (nv_ready, G))

            def store(g):
                wait(sp, fin_copied, g + 1)
                sp.dma_start(out[bass.ds(g * GB, GB)].rearrange("b t c -> t b c"),
                             result_sb[:, step_cols(g)].rearrange("p (b c) -> p b c", b=GB)).then_inc(stored, 16)

            for b in range(GB):
                load_cv(1, b, (v_ready, 8 * G + 3 + b))
            with sp.Fori(2, G) as g:
                for b in range(GB):
                    load_cv(g, b, (v_ready, 4 * g + (8 * G - 1 + b)))
                store(g - 2)
            for g in range(G - 2, G):
                store(g)
            sp.wait_ge(stored, 16 * G)

        @block.gpsimd
        def _(pool):
            pool.memset(mrow[:, :], 0.0).then_inc(zeroed, 1)
            pool.memset(idx_i[:, :, :], 0).then_inc(zeroed, 1)
            pool.memset(ident[:, :], 0.0).then_inc(zeroed, 1)
            pool.wait_ge(zeroed, 3)
            pool.affine_select(out=ident[:, :], in_=ident[:, :], compare_op=ALU.not_equal, fill=1.0, base=0,
                               pattern=[[-1, P]], channel_multiplier=1).then_inc(ident_ready, 1)
            pool.iota(iota_i[:, :], pattern=[[1, T]], base=0, channel_multiplier=0).then_inc(ident_ready, 1)
            pool.memset(mean_w[:, :], 1.0 / C).then_inc(ident_ready, 1)

            pool.wait_ge(ident_ready, 3)
            cleared = [0]

            def clear(ap):
                cleared[0] += 1
                pool.memset(ap.bitcast(F32), 0.0).then_inc(k_cleared, 1)
                pool.wait_ge(k_cleared, cleared[0])

            for k in (k_h, k_l):
                clear(k[64:128, :, 0, :])
                clear(k[0:64, :, 1, :])

            pool.wait_ge(setup_t, 12)
            pool.memset(sq[:, 0:8 * P + REP * C], 0.0).then_inc(zeroed, 1)

            def norm(n, ring):
                wait(pool, rden_ready, n + 1)
                p = probs[:, ring, :, :]
                pool.tensor_tensor(p, p, rden[:, ring, :].unsqueeze(2).to_broadcast([P, 4, T]), ALU.mult)\
                    .then_inc(norm_done, 1)

            def squares(t, g):
                wait(pool, x_updated, t)
                xg = xT[:, step_cols(g)]
                pool.tensor_tensor(sq[:, step_cols(g)], xg, xg, ALU.mult).then_inc(sq_ready, 1)

            def clear_parity(t, e, after):
                wait(pool, scores_ready, 8 * t + after)
                for k in (k_hf, k_lf):
                    clear(k[:, NK_AT[e]:NK_AT[e] + NK])

            def steps(first, last, with_squares=False):
                with pool.Fori(first, last) as t:
                    for u in range(SLOTS):
                        norm(8 * t + u, u % 4)
                        if with_squares and u == UPDATE_AT + 1:
                            squares(t, t - (G + 1))

            def step_clearing(t, clearing, with_squares):
                for u in range(SLOTS):
                    norm(8 * t + u, u % 4)
                    for at, tt, e, after in clearing:
                        if u == at:
                            clear_parity(tt, e, after)
                    if with_squares and u == UPDATE_AT + 1:
                        squares(t, t - (G + 1))

            steps(0, G + 1)
            steps(G + 1, NARROW_AT - 1, with_squares=True)
            step_clearing(NARROW_AT - 1, [(1, NARROW_AT - 1, 0, 2)], True)
            step_clearing(NARROW_AT, [(0, NARROW_AT, 1, 0)], True)
            steps(NARROW_AT + 1, LAST_AT - 1)
            step_clearing(LAST_AT - 1, [(0, LAST_AT - 1, 0, 0)], False)
            step_clearing(LAST_AT, [(0, LAST_AT, 1, 0)], False)
            steps(LAST_AT + 1, 4 * G)

        @block.tensor
        def _(pe):
            def three(out_ap, lhs, rhs, first, last):
                (a_h, a_l), (b_h, b_l) = lhs, rhs
                pe.matmul(out_ap, a_h, b_l, start=first, stop=False, skip_group_check=True)
                pe.matmul(out_ap, a_l, b_h, start=False, stop=False, skip_group_check=True)
                return pe.matmul(out_ap, a_h, b_h, start=False, stop=last, skip_group_check=True)

            pe.wait_ge(ident_ready, 1)
            for i in range(12):
                if i == 0:
                    pe.wait_ge(ctx_loaded[0], 16)
                elif i == 4:
                    pe.wait_ge(ctx_loaded[1], 16)
                elif i == 8:
                    pe.wait_ge(x_loaded, 16)
                if i >= 6:
                    pe.wait_ge(setup_hi, i - 5)
                    pe.wait_ge(setup_lo, i - 5)
                for j in range(4):
                    if i < 8:
                        b, k = 4 * (i // 2) + j, i % 2
                        src = ctx_raw[b // 8][:, (b % 8) * CT + k * P:(b % 8) * CT + (k + 1) * P]
                    else:
                        b = 4 * (i - 8) + j
                        src = x_raw[:, b * C:(b + 1) * C]
                    mm = pe.transpose(setup_banks[i % 6][:, j * P:(j + 1) * P], src, ident[:, :])
                mm.then_inc(setup_t, 1)

            pe.wait_ge(rows_ready, 1)
            pe.matmul(ps_t[:, 0:WIDE * T], alpha[:, :], sel[:, :, :].rearrange("p l t -> p (l t)"), start=True,
                      stop=True).then_inc(bias_made, 1)

            def weights_wait(chunks):
                pe.wait_ge(w_hi, chunks)
                pe.wait_ge(w_lo, chunks)

            def k_piece(s, g, jj):
                wait(pe, k_hi, 4 * s + jj)
                wait(pe, k_lo, 4 * s + jj)
                for p in range(2):
                    for k in range(KT):
                        at = jj * CHUNK + k * 256 + p * P
                        mm = three(ps_k[:, p * GT:(p + 1) * GT],
                                   (w_h[:, at:at + P], w_l[:, at:at + P]),
                                   (c_h[:, k, step_cols(g)], c_l[:, k, step_cols(g)]), k == 0, k == KT - 1)
                mm.then_inc(k_ready, 1)

            def q_piece(t, s, jj):
                wait(pe, q_hi, 4 * s + jj)
                wait(pe, q_lo, 4 * s + jj)
                wait(pe, xs_hi, t + 1)
                wait(pe, xs_lo, t + 1)
                for p in range(2):
                    at = jj * CHUNK + 2 * 256 + p * P
                    mm = three(ps_q[:, p * GT:(p + 1) * GT], (w_h[:, at:at + P], w_l[:, at:at + P]),
                               (xs_h[:, :], xs_l[:, :]), True, True)
                mm.then_inc(q_ready, 1)

            def v_piece(t, s, i):
                b, half = i % 2, i // 2
                wait(pe, v_copied, 4 * s + i)
                wait(pe, cv_loaded[b], 32 * (t + 1))
                for k in range(KT):
                    at = WV0 + half * KT * 512 + k * 512
                    mm = three(ps_v[:, :], (cv_h[:, b, k, :], cv_l[:, b, k, :]),
                               (w_h[:, at:at + 512], w_l[:, at:at + 512]), k == 0, k == KT - 1)
                mm.then_inc(v_ready, 1)

            def nk_piece(g):
                wait(pe, nk_hi, g)
                wait(pe, nk_lo, g)
                for k in range(KT):
                    mm = three(ps_k[:, 0:GT], (nw_h[:, 4 + k, :], nw_l[:, 4 + k, :]),
                               (c_h[:, k, step_cols(g)], c_l[:, k, step_cols(g)]), k == 0, k == KT - 1)
                mm.then_inc(nk_ready, 1)

            def nq_piece(t, g, half):
                wait(pe, nq_hi, 2 * g + half)
                wait(pe, nq_lo, 2 * g + half)
                wait(pe, xs_hi, t + 1)
                wait(pe, xs_lo, t + 1)
                for i in range(2):
                    r = 2 * half + i
                    mm = three(ps_q[:, i * GT:(i + 1) * GT], (nw_h[:, r, :], nw_l[:, r, :]),
                               (xs_h[:, :], xs_l[:, :]), True, True)
                mm.then_inc(nq_ready, 1)

            def nv_piece(t, g):
                wait(pe, nv_copied, g)
                for b in range(GB):
                    wait(pe, cv_loaded[b], 32 * (t + 1))
                    for k in range(KT):
                        mm = three(ps_v[:, b * P:(b + 1) * P], (cv_h[:, b, k, :], cv_l[:, b, k, :]),
                                   (nw_h[:, 6 + k, :], nw_l[:, 6 + k, :]), k == 0, k == KT - 1)
                mm.then_inc(nv_ready, 1)

            def scores_wide(n, s, u):
                jj, b = u // 2, u % 2
                wait(pe, exp_done, n - 1)
                if b == 0:
                    for part in (k_hi, k_lo, q_hi, q_lo):
                        wait(pe, part, 4 * s + jj + 1)
                for p in range(2):
                    pair, tok = 2 * jj + p, slice(b * T, (b + 1) * T)
                    mm = three(ps_s[u % 2][:, p * 2 * T:(p + 1) * 2 * T].rearrange("p (h t) -> p h t", h=2),
                               (q_h[:, pair, tok], q_l[:, pair, tok]),
                               (k_h[:, pair, :, tok], k_l[:, pair, :, tok]), True, True)
                mm.then_inc(scores_ready, 1)

            def scores_narrow(n, g, e, u):
                r, b = u // 2, u % 2
                wait(pe, exp_done, n - 1)
                if u == 0:
                    wait(pe, nk_hi, g + 1)
                    wait(pe, nk_lo, g + 1)
                if u in (0, 4):
                    wait(pe, nq_hi, 2 * g + u // 4 + 1)
                    wait(pe, nq_lo, 2 * g + u // 4 + 1)
                tok = slice(b * T, (b + 1) * T)
                three(ps_s[u % 2][:, :].rearrange("p (h t) -> p h t", h=4),
                      (nq_h[e][:, r, tok], nq_l[e][:, r, tok]),
                      (nk_h[e][:, :, tok], nk_l[e][:, :, tok]), True, True).then_inc(scores_ready, 1)

            def transposes(n, u):
                wait(pe, norm_done, n + 1)
                wait(pe, pt_copied, n)
                for h in range(4):
                    mm = pe.transpose(ps_t[:, h * T:(h + 1) * T], probs[:, u % 4, h, :], ident[:, :])
                mm.then_inc(pt_ready, 1)

            def weigh(n, u, kind, e, v_count):
                wait(pe, pt_copied, n + 1)
                wait(pe, o_hi, n)
                wait(pe, o_lo, n)
                wait(pe, v_copied if kind == "wide" else nv_copied, v_count)
                jj, b = u // 2, u % 2
                for h in range(4):
                    if kind == "wide":
                        a, p = h % 2, h // 2
                        at = (4 * jj + h) * HD
                        mm = pe.matmul(ps_o[a * HD:(a + 1) * HD, p * T:(p + 1) * T], v_sb[:, b, at:at + HD],
                                       probsT[:, u % 2, h, :], start=True, stop=True)
                    else:
                        mm = pe.matmul(ps_o[32 * h:32 * h + 32, 0:T], nv[e][:, b, 32 * h:32 * h + 32],
                                       probsT[:, u % 2, h, :], start=True, stop=True)
                mm.then_inc(o_ready, 1)

            def y_piece(t, jj, kind, n_wo):
                wait(pe, o_hi, 8 * t + 2 * jj + 2)
                wait(pe, o_lo, 8 * t + 2 * jj + 2)
                if jj == 0:
                    wait(pe, x_updated, t)
                if kind == "wide":
                    pe.wait_ge(wo_hi, n_wo)
                    pe.wait_ge(wo_lo, n_wo)
                    for a in range(2):
                        mm = three(ps_y[:, 0:GT], (wo_h[:, 2 * jj + a, :], wo_l[:, 2 * jj + a, :]),
                                   (o_h[:, jj % 2, a, :], o_l[:, jj % 2, a, :]), jj + a == 0, jj + a == 4)
                else:
                    mm = three(ps_y[:, 0:GT], (nwo_h[:, jj, :], nwo_l[:, jj, :]),
                               (o_h[:, jj % 2, 0, :], o_l[:, jj % 2, 0, :]), jj == 0, jj == 3)
                mm.then_inc(y_ready, 1)

            def means(first, last):
                pe.wait_ge(sq_ready, (last + 1) // GB)
                for b in range(first, last):
                    mm = pe.matmul(ps_k[:, b:b + 1], sq[:, b * T:(b + 1) * T], mean_w[:, :], start=True, stop=True)
                mm.then_inc(mean_ready, 1)

            def result(g):
                wait(pe, x_updated, g + (LAST_AT + 1))
                for b in range(GB):
                    mm = pe.transpose(ps_v[:, b * P:(b + 1) * P], last_x[:, b * T:(b + 1) * T], ident[:, :])
                mm.then_inc(fin_t, 1)

            def step(t, s, g, layer, prv, cur, nxt, e=None):
                first = isinstance(s, int) and isinstance(g, int) and g == 0
                last = isinstance(g, int) and g == G - 1
                if e is None and cur == "narrow":
                    e = g % 2
                s_next = s + (cur == "wide")
                g_next = 0 if last else g + 1
                for u in range(SLOTS):
                    n = 8 * t + u
                    if cur == "wide":
                        scores_wide(n, s, u)
                    else:
                        scores_narrow(n, g, e, u)
                    if not (prv is None and u < TLAG):
                        transposes(n - TLAG, (u - TLAG) % 8)
                    for what, i, ahead in pieces(u, cur, nxt):
                        if what == "k":
                            if first and not ahead:
                                weights_wait(6 * layer + i + 1)
                            elif ahead and last:
                                weights_wait(6 * (layer + 1 if cur == "wide" else 2) + i + 1)
                            if cur == "narrow" and i == 0:
                                pe.wait_ge(nk_hi, G)
                                pe.wait_ge(nk_lo, G)
                            k_piece(s_next if ahead else s, g_next if ahead else g, i)
                        elif what == "q":
                            if first and not ahead:
                                weights_wait(6 * layer + i + 1)
                            elif ahead and last:
                                weights_wait(6 * (layer + 1 if cur == "wide" else 2) + i + 1)
                            if cur == "narrow" and i == 0:
                                pe.wait_ge(nq_hi, 2 * G)
                                pe.wait_ge(nq_lo, 2 * G)
                            q_piece(t + ahead, s_next if ahead else s, i)
                        elif what == "v":
                            if first:
                                weights_wait(6 * layer + 5 + i // 2)
                            if i == 0 and prv == "narrow":
                                pe.wait_ge(nv_copied, G)
                            if i == 3 and layer == 2 and not first:
                                wait(pe, fin_copied, g)
                            v_piece(t, s, i)
                        elif what == "nk":
                            if cur == "wide":
                                pe.wait_ge(k_hi, 8 * G)
                                pe.wait_ge(k_lo, 8 * G)
                                pe.wait_ge(nw_hi, 2)
                                pe.wait_ge(nw_lo, 2)
                            else:
                                pe.wait_ge(root_ready, 1 if isinstance(t, int) and t < NARROW_AT + 2 else 2)
                            nk_piece(g_next)
                        elif what == "nq":
                            if cur == "wide" and i == 0:
                                pe.wait_ge(q_hi, 8 * G)
                                pe.wait_ge(q_lo, 8 * G)
                            nq_piece(t + 1, g_next, i)
                        elif what == "nv":
                            if first:
                                pe.wait_ge(v_copied, 8 * G)
                            nv_piece(t, g)
                    if u == MEAN_AT and isinstance(t, int) and t == NARROW_AT - 1:
                        pe.wait_ge(nk_hi, 1)
                        pe.wait_ge(nk_lo, 1)
                        means(0, EARLY)
                    if u == MEAN_AT and isinstance(t, int) and t == NARROW_AT + 1:
                        pe.wait_ge(nk_hi, 3)
                        pe.wait_ge(nk_lo, 3)
                        means(EARLY, B)
                    if u % 2 == 0 and (u == 6 or prv):
                        jj = (u // 2 + 1) % 4
                        if u == 6:
                            y_piece(t, 0, cur, None if layer is None else 4 * layer + 1 if first
                                    else 4 * layer + 4)
                        else:
                            y_piece(t - 1, jj, prv, 4 * (layer + 1) if layer is not None and not first
                                    else 4 * layer if layer is not None and prv == "wide" else 8)
                    if not (prv is None and u < PLAG):
                        m = u - PLAG
                        kind = cur if m >= 0 else prv
                        if kind == "wide":
                            count = 4 * s + (2 * (m // 4) + m % 2 + 1 if m >= 0 else 0)
                        else:
                            count = g + 1 if m >= 0 else (G if cur == "wide" else g)
                        weigh(n - PLAG, m % 8, kind, e if m >= 0 else (1 if cur == "wide" else 1 - (e or 0)),
                              count)
                    if layer == 2 and u == UPDATE_AT + 1 and not first:
                        wait(pe, v_copied, 4 * s + 3)
                        result(g - 1)

            pe.wait_ge(setup_hi, 12)
            pe.wait_ge(setup_lo, 8)
            for what, i in FIRST_PIECES:
                weights_wait(i + 1)
                if what == "k":
                    k_piece(0, 0, i)
                else:
                    q_piece(0, 0, i)
            pe.wait_ge(k_cleared, 4)
            pe.wait_ge(bias_ready, 1)
            walk(pe, step)
            t = 4 * G
            for m in (2, 1):
                transposes(8 * t - m, 8 - m)
                if m == 2:
                    y_piece(t - 1, 1, "wide", 12)
                weigh(8 * t - m - 1, 7 - m, "wide", None, 12 * G)
            weigh(8 * t - 1, 7, "wide", None, 12 * G)
            y_piece(t - 1, 2, "wide", 12)
            y_piece(t - 1, 3, "wide", 12)
            pe.wait_ge(fin_copied, G - 1)
            result(G - 1)

        @block.scalar
        def _(act):
            act.dma_start(x_raw.rearrange("p (b c) -> p b c", c=C), x.rearrange("b t c -> t b c"))\
               .then_inc(x_loaded, 16)
            for i in range(12):
                act.wait_ge(setup_t, i + 1)
                if i < 8:
                    dst = c_h[:, i % 2, 512 * (i // 2):512 * (i // 2) + 512]
                else:
                    dst = xT[:, 512 * (i - 8):512 * (i - 8) + 512]
                act.activation(dst, setup_banks[i % 6][:, :], ACT.Copy).then_inc(setup_hi, 1)

            def split(layer, c):
                act.wait_ge(w_loaded[c], (32 if c < 4 else 16) * (layer + 1))
                act.activation(chunk(w_h, c), raw(layer, c), ACT.Copy).then_inc(w_hi, 1)

            def split_wo(layer, part):
                act.wait_ge(wo_loaded[part], 16 * (layer + 1))
                a = slice(2 * part, 2 * part + 2)
                act.activation(wo_h[:, a, :], wo_raw[:, part % 2, :, :], ACT.Copy).then_inc(wo_hi, 1)

            def split_narrow():
                act.wait_ge(columns_loaded, 16 * 2)
                act.wait_ge(narrow_loaded, 16 * (REP * 5 + 4))
                act.activation(nw_h[:, :, :], nw_raw, ACT.Copy).then_inc(nw_hi, 1)
                act.activation(nwo_h[:, :, :], nwo_raw, ACT.Copy).then_inc(nw_hi, 1)

            def split_x(g, kind, after, used):
                wait(act, x_updated, after)
                if used is not None:
                    wait(act, used[0], used[1])
                if kind == "wide":
                    act.activation(xs_h[:, :], xT[:, step_cols(g)], ACT.Copy).then_inc(xs_hi, 1)
                else:
                    act.activation(xs_h[:, :], xT[:, step_cols(g)], ACT.Identity, scale=nw_sb[:, 0:1])\
                       .then_inc(xs_hi, 1)

            def k_upper(s, jj):
                wait(act, k_ready, 4 * s + jj + 1)
                src = ps_k[:, :].rearrange("p (a t) -> p a t", a=2)
                for half in range(2):
                    rows = slice(64 * half, 64 * half + 64)
                    last = act.activation(k_h[rows, 2 * jj:2 * jj + 2, half, :], src[rows], ACT.Copy)
                last.then_inc(k_hi, 1)

            def q_upper(s, jj):
                wait(act, q_ready, 4 * s + jj + 1)
                act.activation(q_h[:, 2 * jj:2 * jj + 2, :], ps_q[:, :].rearrange("p (a t) -> p a t", a=2),
                               ACT.Copy, scale=-HD ** -0.5).then_inc(q_hi, 1)

            def v_copy(s, i):
                wait(act, v_ready, 4 * s + i + 1)
                act.activation(v_sb[:, i % 2, 512 * (i // 2):512 * (i // 2) + 512], ps_v[:, :], ACT.Copy)\
                   .then_inc(v_copied, 1)

            def nk_upper(g, e):
                wait(act, nk_ready, g + 1)
                for h in range(KV):
                    rows = slice(32 * h, 32 * h + 32)
                    last = act.activation(nk_h[e][rows, h, :], ps_k[rows, 0:GT], ACT.Copy)
                last.then_inc(nk_hi, 1)

            def nq_upper(g, e, half):
                wait(act, nq_ready, 2 * g + half + 1)
                act.activation(nq_h[e][:, 2 * half:2 * half + 2, :],
                               ps_q[:, :].rearrange("p (a t) -> p a t", a=2), ACT.Copy,
                               scale=RD ** -0.5).then_inc(nq_hi, 1)

            def nv_copy(g, e):
                wait(act, nv_ready, g + 1)
                act.activation(nv[e], ps_v[:, 0:GB * P].rearrange("p (b n) -> p b n", b=GB), ACT.Copy)\
                   .then_inc(nv_copied, 1)

            def roots(first, last, count):
                act.wait_ge(mean_ready, count)
                act.activation(root[:, first:last], ps_k[:, first:last], ACT.Sqrt, bias=eps_sb[:, :])\
                   .then_inc(root_ready, 1)

            def result_copy(g):
                wait(act, fin_t, g + 1)
                act.activation(result_sb[:, step_cols(g)], ps_v[:, 0:GB * C], ACT.Copy).then_inc(fin_copied, 1)

            def exps(n, u, kind, e):
                wait(act, max_ready, n + 1)
                wait(act, pt_ready, n - 3)
                scale = -1.0 if kind == "wide" else inv[:, e, u % 2:u % 2 + 1]
                for h in range(4):
                    last = act.activation(probs[:, u % 4, h, :], ps_s[u % 2][:, h * T:(h + 1) * T], ACT.Exp,
                                          scale=scale, bias=nmax[:, u % 4, h:h + 1],
                                          accum_out=den[:, u % 4, h:h + 1])
                last.then_inc(exp_done, 1)

            def o_upper(t, n, m, kind):
                wait(act, o_ready, n + 1)
                wait(act, y_ready, 4 * t + m // 2 - 1)
                jj, b = m % 8 // 2, m % 2
                if kind == "wide":
                    act.activation(o_h[:, jj % 2, :, b * T:(b + 1) * T],
                                   ps_o[:, 0:2 * T].rearrange("p (a t) -> p a t", a=2), ACT.Copy)\
                       .then_inc(o_hi, 1)
                else:
                    act.activation(o_h[:, jj % 2, 0, b * T:(b + 1) * T], ps_o[:, 0:T], ACT.Copy)\
                       .then_inc(o_hi, 1)

            def upper(s, s_next, g_next, e_next, g, e, found, clears):
                for what, i, ahead in found:
                    if what in clears and i == clears[what][0]:
                        act.wait_ge(k_cleared, clears[what][1])
                    if what == "k":
                        k_upper(s_next if ahead else s, i)
                    elif what == "q":
                        q_upper(s_next if ahead else s, i)
                    elif what == "v":
                        v_copy(s, i)
                    elif what == "nk":
                        nk_upper(g_next, e_next)
                    elif what == "nq":
                        nq_upper(g_next, e_next, i)
                    elif what == "nv":
                        nv_copy(g, e)

            def step(t, s, g, layer, prv, cur, nxt, e=None):
                last = isinstance(g, int) and g == G - 1
                known = isinstance(t, int)
                if e is None:
                    e = g % 2 if cur == "narrow" else 1
                s_next = s + (cur == "wide")
                g_next = 0 if last else g + 1
                e_next = 0 if cur == "wide" else 1 - e
                clears = {NARROW_AT - 1: {"nk": (0, 6)}, NARROW_AT: {"nk": (0, 8)}, LAST_AT - 1: {"k": (0, 10)},
                          LAST_AT: {"k": (3, 12)}}.get(t, {}) if known else {}
                for u in range(SLOTS):
                    n, m = 8 * t + u, u - OLAG
                    if not (prv is None and m < 0):
                        o_upper(t, n - OLAG, m, cur if m >= 0 else prv)
                    if layer == 2 and u == UPDATE_AT + 2 and not (known and g == 0):
                        result_copy(g - 1)
                    if u:
                        upper(s, s_next, g_next, e_next, g, e, pieces(u - 1, cur, nxt), clears)
                    elif prv:
                        upper(s - 1, s, g, e, g, e, pieces(7, prv, cur), {})
                    if known and t in (G - 1, NARROW_AT - 1) and u in REFRESH:
                        split(layer + 1, REFRESH[u])
                    if known and t == 0:
                        if u == 0:
                            for c in range(3, 5):
                                split(0, c)
                        if u == REFRESH_5:
                            split(0, 5)
                        if u in REFRESH_WO:
                            split_wo(0, REFRESH_WO[u])
                        if u == SLOTS - 1:
                            split_narrow()
                    if known and t in (G, NARROW_AT):
                        if u == REFRESH_5:
                            split(t // G, 5)
                        if u in REFRESH_WO:
                            split_wo(t // G, REFRESH_WO[u])
                    if u == XS_AT and nxt:
                        if cur == "wide":
                            used = (q_ready, 4 * s + 4)
                        else:
                            used = (nq_ready, 2 * g + 2)
                        split_x(g_next, nxt, 0 if layer == 0 and not last else t - 6, used)
                    if u == MEAN_AT + 1 and known and t == NARROW_AT - 1:
                        roots(0, EARLY, 1)
                    if u == MEAN_AT + 1 and known and t == NARROW_AT + 1:
                        roots(EARLY, B, 2)
                    exps(n, u, cur, e)

            act.wait_ge(setup_hi, 12)
            for c in range(3):
                split(0, c)
                if c == 0:
                    split_x(0, "wide", 0, None)
                if c == 1:
                    for what, i in FIRST_PIECES:
                        (k_upper if what == "k" else q_upper)(0, i)
            walk(act, step)
            v_copy(3 * G - 1, 3)
            for m in range(OLAG, 0, -1):
                o_upper(4 * G, 32 * G - m, -m, "wide")
            result_copy(G - 1)

        @block.vector
        def _(dve):
            done = [0]

            def then(ins):
                done[0] += 1
                ins.then_inc(rows_step, 1)
                dve.wait_ge(rows_step, done[0])

            then(dve.memset(alpha[:, :].bitcast(F32), 0.0))
            then(dve.memset(sel[:, :, :].bitcast(F32), 0.0))
            then(dve.memset(flag[:, :], 0.0))
            then(dve.memset(flag[0:1, :], 1.0))
            then(dve.memset(flag[32:33, :], 1.0))
            then(dve.memset(eps_sb[:, :], EPS))
            dve.wait_ge(small_loaded, 16 * 8)
            then(dve.tensor_scalar(mrow[:, :], mrow[:, :], -1.0, 1.0, ALU.mult, ALU.add))
            then(dve.tensor_scalar(mrow[:, :], mrow[:, :], SUPPRESS, None, ALU.mult))
            then(dve.tensor_copy(mhi[:, :], mrow[:, :]))
            then(dve.tensor_copy(alpha[0:2, :], mrow[0:2, :]))
            then(dve.tensor_tensor(alpha[32:34, :], mrow[32:34, :], mhi[32:34, :].bitcast(F32), ALU.subtract))
            dve.wait_ge(ident_ready, 2)
            then(dve.tensor_copy(iota_f[:, :], iota_i[:, :]))
            src = idx_i[:, :, :].rearrange("p l (k c) -> p l k c", k=2)
            then(dve.tensor_copy(idx_f[:, :, :, 0:2], src))
            then(dve.tensor_scalar(idx_f[:, :, :, 2:4], idx_f[:, :, :, 0:2], float(T), None, ALU.add))
            for layer in range(WIDE):
                for k in range(2):
                    hit = ps_o[0:64, :].rearrange("p (j t) -> p j t", j=4)
                    then(dve.tensor_tensor(hit, iota_f[:, :].unsqueeze(1).to_broadcast([64, 4, T]),
                                           idx_f[:, layer, k, :].unsqueeze(2).to_broadcast([64, 4, T]),
                                           ALU.is_equal))
                    then(dve.tensor_reduce(picked[:, k, :], hit.rearrange("p j t -> p t j"), AX.X, ALU.max))
                then(dve.scalar_tensor_tensor(out=both[:, :], in0=picked[:, 1, :], scalar=flag[:, 0:1],
                                              in1=picked[:, 0, :], op0=ALU.mult, op1=ALU.mult))
                then(dve.tensor_tensor(sel[0:64, layer, :], picked[:, 0, :], both[:, :], ALU.subtract))
            dve.memset(flag[:, :], 0.0).then_inc(rows_ready, 1)

            for i in range(8):
                dve.wait_ge(setup_hi, i + 1)
                cols = slice(512 * (i // 2), 512 * (i // 2) + 512)
                dve.tensor_tensor(c_l[:, i % 2, cols], setup_banks[i % 6][:, :],
                                  c_h[:, i % 2, cols].bitcast(F32), ALU.subtract).then_inc(setup_lo, 1)

            def split(layer, c):
                dve.wait_ge(w_hi, 6 * layer + c + 1)
                dve.tensor_tensor(chunk(w_l, c), raw(layer, c), chunk(w_h, c).bitcast(F32),
                                  ALU.subtract).then_inc(w_lo, 1)

            def split_wo(layer, part):
                dve.wait_ge(wo_hi, 4 * layer + part + 1)
                a = slice(2 * part, 2 * part + 2)
                dve.tensor_tensor(wo_l[:, a, :], wo_raw[:, part % 2, :, :], wo_h[:, a, :].bitcast(F32),
                                  ALU.subtract).then_inc(wo_lo, 1)

            def split_narrow():
                for i, (came, high, low) in enumerate(((nw_raw, nw_h, nw_l), (nwo_raw, nwo_h, nwo_l))):
                    dve.wait_ge(nw_hi, i + 1)
                    dve.tensor_tensor(low[:, :, :], came, high[:, :, :].bitcast(F32), ALU.subtract)\
                       .then_inc(nw_lo, 1)

            def split_x(t, g, kind):
                wait(dve, xs_hi, t + 1)
                if kind == "wide":
                    dve.tensor_tensor(xs_l[:, :], xT[:, step_cols(g)], xs_h[:, :].bitcast(F32), ALU.subtract)\
                       .then_inc(xs_lo, 1)
                else:
                    dve.scalar_tensor_tensor(out=xs_l[:, :], in0=xT[:, step_cols(g)], scalar=nw_sb[:, 0:1],
                                             in1=xs_h[:, :].bitcast(F32), op0=ALU.mult, op1=ALU.subtract)\
                       .then_inc(xs_lo, 1)

            def k_lower(s, jj):
                wait(dve, k_hi, 4 * s + jj + 1)
                src = ps_k[:, :].rearrange("p (a t) -> p a t", a=2)
                for half in range(2):
                    rows = slice(64 * half, 64 * half + 64)
                    pair = slice(2 * jj, 2 * jj + 2)
                    last = dve.tensor_tensor(k_l[rows, pair, half, :], src[rows],
                                             k_h[rows, pair, half, :].bitcast(F32), ALU.subtract)
                last.then_inc(k_lo, 1)

            def q_lower(s, jj):
                wait(dve, q_hi, 4 * s + jj + 1)
                pair = slice(2 * jj, 2 * jj + 2)
                dve.scalar_tensor_tensor(out=q_l[:, pair, :], in0=ps_q[:, :].rearrange("p (a t) -> p a t", a=2),
                                         scalar=-HD ** -0.5, in1=q_h[:, pair, :].bitcast(F32), op0=ALU.mult,
                                         op1=ALU.subtract).then_inc(q_lo, 1)

            def nk_lower(g, e):
                wait(dve, nk_hi, g + 1)
                for h in range(KV):
                    rows = slice(32 * h, 32 * h + 32)
                    last = dve.tensor_tensor(nk_l[e][rows, h, :], ps_k[rows, 0:GT],
                                             nk_h[e][rows, h, :].bitcast(F32), ALU.subtract)
                last.then_inc(nk_lo, 1)

            def nq_lower(g, e, half):
                wait(dve, nq_hi, 2 * g + half + 1)
                r = slice(2 * half, 2 * half + 2)
                dve.scalar_tensor_tensor(out=nq_l[e][:, r, :], in0=ps_q[:, :].rearrange("p (a t) -> p a t", a=2),
                                         scalar=RD ** -0.5, in1=nq_h[e][:, r, :].bitcast(F32), op0=ALU.mult,
                                         op1=ALU.subtract).then_inc(nq_lo, 1)

            def update_x(t, g, layer):
                wait(dve, y_ready, 4 * t + 4)
                xg = xT[:, step_cols(g)]
                if layer is None:
                    dve.tensor_tensor(xg, ps_y[:, 0:GT], xg, ALU.add).then_inc(x_updated, 1)
                else:
                    dve.scalar_tensor_tensor(out=xg if layer < 2 else last_x[:, :], in0=ps_y[:, 0:GT],
                                             scalar=bo_sb[:, layer:layer + 1], in1=xg, op0=ALU.add,
                                             op1=ALU.add).then_inc(x_updated, 1)

            def minima(n, u, layer):
                wait(dve, scores_ready, n + 1)
                dve.memset(gate[:, :], 0.0)
                for h in range(4):
                    sc = ps_s[u % 2][:, h * T:(h + 1) * T]
                    last = dve.tensor_tensor_reduce(sc, sc, bias[:, layer, :], 1.0, FAR, ALU.add, ALU.min,
                                                    nmax[:, u % 4, h:h + 1])
                last.then_inc(max_ready, 1)

            def maxima(n, u):
                wait(dve, scores_ready, n + 1)
                dve.tensor_reduce(peak[:, u % 4, :], ps_s[u % 2][:, :].rearrange("p (h t) -> p h t", h=4),
                                  AX.X, ALU.max, negate=True).then_inc(peak_ready, 1)

            def scale_maxima(g, u, e):
                wait(dve, peak_ready, 8 * g + u + 1)
                dve.tensor_scalar(nmax[:, u % 4, :], peak[:, u % 4, :], inv[:, e, u % 2:u % 2 + 1], None,
                                  ALU.mult).then_inc(max_ready, 1)

            def sums(n, u):
                wait(dve, exp_done, n + 1)
                dve.reciprocal(rden[:, u % 4, :], den[:, u % 4, :]).then_inc(rden_ready, 1)

            def pt_copy(n, u):
                wait(dve, pt_ready, n + 1)
                wait(dve, o_ready, n - 1)
                dve.tensor_copy(probsT[:, u % 2, :, :], ps_t[:, :].rearrange("p (h t) -> p h t", h=4))\
                   .then_inc(pt_copied, 1)

            def o_lower(n, m, kind):
                wait(dve, o_hi, n + 1)
                jj, b = m % 8 // 2, m % 2
                if kind == "wide":
                    tok = slice(b * T, (b + 1) * T)
                    dve.tensor_tensor(o_l[:, jj % 2, :, tok], ps_o[:, 0:2 * T].rearrange("p (a t) -> p a t", a=2),
                                      o_h[:, jj % 2, :, tok].bitcast(F32), ALU.subtract).then_inc(o_lo, 1)
                else:
                    tok = slice(b * T, (b + 1) * T)
                    dve.tensor_tensor(o_l[:, jj % 2, 0, tok], ps_o[:, 0:T],
                                      o_h[:, jj % 2, 0, tok].bitcast(F32), ALU.subtract).then_inc(o_lo, 1)

            def lower(s, s_next, g_next, e_next, found):
                for what, i, ahead in found:
                    if what == "k":
                        k_lower(s_next if ahead else s, i)
                    elif what == "q":
                        q_lower(s_next if ahead else s, i)
                    elif what == "nk":
                        nk_lower(g_next, e_next)
                    elif what == "nq":
                        nq_lower(g_next, e_next, i)

            def step(t, s, g, layer, prv, cur, nxt, e=None):
                first = isinstance(g, int) and g == 0
                last = isinstance(g, int) and g == G - 1
                known = isinstance(t, int)
                if e is None:
                    e = g % 2 if cur == "narrow" else 1
                s_next = s + (cur == "wide")
                g_next = 0 if last else g + 1
                e_next = 0 if cur == "wide" else 1 - e
                for u in range(SLOTS):
                    n = 8 * t + u
                    if cur == "wide":
                        if not (prv is None and u < 1):
                            sums(n - 1, (u - 1) % 8)
                        minima(n, u, layer)
                    else:
                        if u == 0:
                            dve.wait_ge(root_ready, 2 if not known or g >= EARLY // GB else 1)
                            dve.reciprocal(inv[:, e, :], root[:, bass.ds(g * GB, GB)]).then_inc(inv_ready, 1)
                        maxima(n, u)
                        sums(n - 1, (u - 1) % 8)
                        if u == 0:
                            wait(dve, inv_ready, g + 1)
                        scale_maxima(g, u, e)
                    m = u - OLAG
                    if not (prv is None and m < 0):
                        o_lower(n - OLAG, m, cur if m >= 0 else prv)
                    if not (prv is None and u < TLAG):
                        pt_copy(n - TLAG, (u - TLAG) % 8)
                    if u == UPDATE_AT and prv:
                        update_x(t - 1, G - 1 if first else g - 1,
                                 (layer if not first else layer - 1) if layer is not None and prv == "wide"
                                 else 1 if prv == "wide" else None)
                    if u:
                        lower(s, s_next, g_next, e_next, pieces(u - 1, cur, nxt))
                    elif prv:
                        lower(s - 1, s, g, e, pieces(7, prv, cur))
                    if known and t in (G - 1, NARROW_AT - 1) and u in REFRESH:
                        split(layer + 1, REFRESH[u])
                    if known and t == 0:
                        if u == 0:
                            for c in range(3, 5):
                                split(0, c)
                        if u == REFRESH_5:
                            split(0, 5)
                        if u in REFRESH_WO:
                            split_wo(0, REFRESH_WO[u])
                        if u == SLOTS - 1:
                            split_narrow()
                    if known and t in (G, NARROW_AT):
                        if u == REFRESH_5:
                            split(t // G, 5)
                        if u in REFRESH_WO:
                            split_wo(t // G, REFRESH_WO[u])
                    if u == XS_AT and nxt:
                        split_x(t + 1, g_next, nxt)

            dve.wait_ge(bias_made, 1)
            dve.tensor_copy(bias[:, :, :].rearrange("p l t -> p (l t)"), ps_t[:, 0:WIDE * T])\
               .then_inc(bias_ready, 1)
            for c in range(3):
                split(0, c)
                if c == 0:
                    split_x(0, 0, "wide")
                if c == 1:
                    for what, i in FIRST_PIECES:
                        (k_lower if what == "k" else q_lower)(0, i)
            dve.wait_ge(columns_loaded, 16 * 2)
            walk(dve, step)
            sums(32 * G - 1, 7)
            o_lower(32 * G - 4, -4, "wide")
            pt_copy(32 * G - 2, 6)
            o_lower(32 * G - 3, -3, "wide")
            pt_copy(32 * G - 1, 7)
            for m in (-2, -1):
                o_lower(32 * G + m, m, "wide")
            update_x(4 * G - 1, G - 1, 2)


def kernel(**inputs):
    import numpy as _np
    import concourse.bacc as _bacc
    from concourse import mybir as _mybir
    from concourse.bass_utils import run_bass_kernel_spmd as _run

    a = {k: _np.asarray(v) for k, v in inputs.items()}
    wide = ("L0", "L1", "L3")

    def stacked(name):
        return _np.stack([a[f"{w}_xattn_{name}"] for w in wide])

    arrays = {
        "x": a["x"], "ctx_in": a["ctx_2048"], "masks": _np.stack([a["mask_S_fk1"], a["mask_S_fk0"]]),
        "tokens": _np.stack([stacked("token_indices_A"), stacked("token_indices_B")], axis=1),
        "wq": stacked("Wq"), "wk": stacked("Wk"), "wv": stacked("Wv"), "wo": stacked("Wo"), "bo": stacked("bo").T,
        "nwq": a["L2_xattn_wq"], "nwk": a["L2_xattn_wk"], "nwv": a["L2_xattn_wv"], "nwo": a["L2_xattn_wo"],
        "nw": a["L2_xattn_norm_w"][:, None],
    }
    arrays = {f"in_{k}": _np.ascontiguousarray(v) for k, v in arrays.items()}
    nc = _bacc.Bacc("TRN2", target_bir_lowering=False, num_devices=1)
    args = [nc.dram_tensor(k, v.shape, _mybir.dt.from_np(v.dtype), kind="ExternalInput").ap()
            for k, v in arrays.items()]
    args.append(nc.dram_tensor("out_x", (B, T, C), _mybir.dt.float32, kind="ExternalOutput").ap())
    build_program(nc, *args)
    r = _run(nc, [arrays], core_ids=[0])
    return r.results[0]["out_x"]
```

```python
from contextlib import ExitStack

import concourse.bass as bass
from concourse import mybir

F32 = mybir.dt.float32
F32R = mybir.dt.float32r
ALU = mybir.AluOpType
ACT = mybir.ActivationFunctionType
AX = mybir.AxisListType

P = 128
B, T, C = 16, 128, 128
CT, KT = 256, 2
HEADS, HD = 16, 64
INNER = HEADS * HD
PAIRS = HEADS // 2
KV, RD = 4, 8
REP = HEADS // KV
GB = 2
G = B // GB
GT = GB * T
SLOTS = 8
SUPPRESS = 20.0
EPS = 1e-5
FAR = 3.4e38
CHUNK = 3 * 256
WV0 = 4 * CHUNK
WCOLS = WV0 + KT * INNER
WIDE = 3
ROWS = 32 * WIDE
NARROW_AT = 2 * G
LAST_AT = 3 * G


def build_program(nc, x, ctx_in, rows, tokens, wq, wk, wv, wo, bo, nw, nwo, norm_w, out):
    with ExitStack() as stack:
        def sb(name, shape, dt=F32):
            return stack.enter_context(nc.sbuf_tensor(name, shape, dt))

        def sem(name):
            return stack.enter_context(nc.semaphore(name))

        xT = sb("xT", [P, B * T])
        xs_h, xs_l = sb("xs_h", [P, GT], F32R), sb("xs_l", [P, GT], F32R)
        c_h, c_l = sb("c_h", [P, KT, B * T], F32R), sb("c_l", [P, KT, B * T], F32R)
        cv_h, cv_l = sb("cv_h", [P, GB, KT, T], F32R), sb("cv_l", [P, GB, KT, T], F32R)
        w_h, w_l = sb("w_h", [P, WCOLS], F32R), sb("w_l", [P, WCOLS], F32R)
        w_raw = sb("w_raw", [P, 2, KT * INNER // 2])
        wo_raw = sb("wo_raw", [P, 2, 2, C])
        wo_h, wo_l = sb("wo_h", [P, PAIRS, C], F32R), sb("wo_l", [P, PAIRS, C], F32R)
        k_h, k_l = sb("k_h", [P, PAIRS, 2, GT], F32R), sb("k_l", [P, PAIRS, 2, GT], F32R)
        q_h, q_l = sb("q_h", [P, PAIRS, GT], F32R), sb("q_l", [P, PAIRS, GT], F32R)
        v_sb = sb("v_sb", [P, GB, INNER])
        o_h, o_l = sb("o_h", [P, 2, 2, GT], F32R), sb("o_l", [P, 2, 2, GT], F32R)
        probs = sb("probs", [P, 4, 4, T])
        probsT = sb("probsT", [P, 2, 4, T])
        nmax = sb("nmax", [P, 4, 4])
        den = sb("den", [P, 4, 4])
        rden = sb("rden", [P, 4, 4])
        ident = sb("ident", [P, P])
        ones = sb("ones", [P, P])
        alpha = sb("alpha", [ROWS, T], F32R)
        sel = sb("sel", [ROWS, WIDE, T], F32R)
        rows_sb = sb("rows_sb", [ROWS, T + 4])
        tok_i = sb("tok_i", [ROWS, 4], mybir.dt.int32)
        tok_f = sb("tok_f", [ROWS, 2, 4])
        bias = sb("bias", [P, WIDE, T])
        bo_sb = sb("bo_sb", [P, WIDE])
        nw_sb = sb("nw_sb", [P, 1])
        eps_sb = sb("eps_sb", [P, 1])
        nw_h, nw_l = sb("nw_h", [P, 8, P], F32R), sb("nw_l", [P, 8, P], F32R)
        nwo_h, nwo_l = sb("nwo_h", [P, REP, C], F32R), sb("nwo_l", [P, REP, C], F32R)
        sq = sb("sq", [P, B * T])
        last_x = sb("last_x", [P, GT])
        xn = last_x
        diag = sq[:, 0:GB * T].rearrange("p (b t) -> p b t", b=GB)
        result_sb = sq
        root = sb("root", [P, B])
        inv = sb("inv", [P, GB])
        gate = sb("gate", [P, 1])
        iota_i = sb("iota_i", [ROWS, T], mybir.dt.int32)
        iota_f = sb("iota_f", [ROWS, T])

        x_raw = sq[:, :]
        nw_raw = sq[:, 0:8 * P].rearrange("p (m n) -> p m n", m=8)
        nwo_raw = sq[:, 8 * P:8 * P + REP * C].rearrange("p (r n) -> p r n", r=REP)
        own, of_b = last_x[0:ROWS, 0:T], last_x[0:ROWS, T:2 * T]
        ctx_raw = [v_sb[:].rearrange("p b n -> p (b n)"), probs[:].rearrange("p r h t -> p (r h t)")]
        k_hf, k_lf = (k[:].rearrange("p a s t -> p (a s t)") for k in (k_h, k_l))
        q_hf, q_lf = (q[:].rearrange("p a t -> p (a t)") for q in (q_h, q_l))
        NK = KV * GT
        NK_AT = [0, 2 * GT * PAIRS - NK]
        nk_h, nk_l = ([k[:, at:at + NK].rearrange("p (g t) -> p g t", g=KV) for at in NK_AT]
                      for k in (k_hf, k_lf))
        nq_h, nq_l = ([q[:, e * REP * GT:(e + 1) * REP * GT].rearrange("p (r t) -> p r t", r=REP)
                       for e in range(2)] for q in (q_hf, q_lf))
        nv = [v_sb[:, e, INNER // 2:INNER // 2 + GB * P].rearrange("p (b n) -> p b n", b=GB) for e in range(2)]

        def bank(name):
            return stack.enter_context(nc.psum_tensor(name, [P, 512], F32))

        ps_s = [bank("ps_s0"), bank("ps_s1")]
        ps_t = bank("ps_t")
        ps_o = bank("ps_o")
        ps_k = bank("ps_k")
        ps_q = bank("ps_q")
        ps_v = bank("ps_v")
        ps_y = bank("ps_y")
        setup_banks = [ps_s[0], ps_s[1], ps_y, ps_v, ps_o]

        scores_ready = sem("scores_ready")
        max_ready = sem("max_ready")
        exp_done = sem("exp_done")
        rden_ready = sem("rden_ready")
        norm_done = sem("norm_done")
        pt_ready = sem("pt_ready")
        pt_copied = sem("pt_copied")
        o_ready = sem("o_ready")
        o_hi, o_lo = sem("o_hi"), sem("o_lo")
        k_ready, k_hi, k_lo = sem("k_ready"), sem("k_hi"), sem("k_lo")
        q_ready, q_hi, q_lo = sem("q_ready"), sem("q_hi"), sem("q_lo")
        v_ready, v_copied = sem("v_ready"), sem("v_copied")
        nk_ready, nk_hi, nk_lo = sem("nk_ready"), sem("nk_hi"), sem("nk_lo")
        nq_ready, nq_hi, nq_lo = sem("nq_ready"), sem("nq_hi"), sem("nq_lo")
        nv_ready, nv_copied = sem("nv_ready"), sem("nv_copied")
        y_ready, x_updated = sem("y_ready"), sem("x_updated")
        xs_hi, xs_lo = sem("xs_hi"), sem("xs_lo")
        cv_loaded = [sem("cv_loaded0"), sem("cv_loaded1")]
        w_loaded = [sem(f"w_loaded{c}") for c in range(6)]
        w_hi, w_lo = sem("w_hi"), sem("w_lo")
        wo_loaded = [sem(f"wo_loaded{part}") for part in range(4)]
        wo_hi, wo_lo = sem("wo_hi"), sem("wo_lo")
        x_loaded = [sem(f"x_loaded{part}") for part in range(4)]
        ctx_loaded = [sem(f"ctx_loaded{part}") for part in range(4)]
        small_loaded, columns_loaded = sem("small_loaded"), sem("columns_loaded")
        narrow_loaded = sem("narrow_loaded")
        zeroed = sem("zeroed")
        ident_ready = sem("ident_ready")
        setup_t, setup_hi, setup_lo = sem("setup_t"), sem("setup_hi"), sem("setup_lo")
        rows_step, rows_ready, bias_made, bias_ready = (sem("rows_step"), sem("rows_ready"), sem("bias_made"),
                                                        sem("bias_ready"))
        nw_hi, nw_lo = sem("nw_hi"), sem("nw_lo")
        k_cleared = sem("k_cleared")
        sq_ready, mean_ready, mean_copied, root_ready = (sem("sq_ready"), sem("mean_ready"), sem("mean_copied"),
                                                         sem("root_ready"))
        inv_ready, diag_ready, spread_ready, xn_ready = (sem("inv_ready"), sem("diag_ready"),
                                                         sem("spread_ready"), sem("xn_ready"))
        fin_t, fin_copied, stored = sem("fin_t"), sem("fin_copied"), sem("stored")

        def wait(eng, semaphore, value):
            if not isinstance(value, int) or value > 0:
                eng.wait_ge(semaphore, value)

        PIECES = {"wide": {0: [("v", 0, 0), ("q", 2, 0)], 1: [("k", 2, 0)], 2: [("v", 1, 0), ("q", 3, 0)],
                           3: [("k", 3, 0)], 4: [("v", 2, 0), ("q", 0, 1)], 5: [("k", 0, 1)],
                           6: [("v", 3, 0), ("q", 1, 1)], 7: [("k", 1, 1)]},
                  "narrow": {0: [("nq", 1, 0)], 2: [("nv", 0, 0)], 4: [("nk", 0, 1)], 5: [("nq", 0, 1)]},
                  "first narrow": {5: [("nk", 0, 1)], 6: [("nq", 0, 1)]}}
        SETUP = [("c", 0, 0), ("c", 0, 1), ("x", 0), ("w", 0), ("xs",), ("rows", 0), ("w", 1), ("k", 0),
                 ("c", 1, 0), ("q", 0), ("rows", 1), ("k", 1), ("c", 1, 1), ("c", 2, 0), ("q", 1), ("c", 2, 1), ("w", 2),
                 ("bias",), ("x", 1), ("c", 3, 0), ("w", 3), ("c", 3, 1), ("w", 4), ("x", 2), ("x", 3)]
        TILES = [item for item in SETUP if item[0] in ("c", "x")]

        def split_by(i):
            return sum(item[0] == "c" for item in TILES[:i])

        TLAG, PLAG, OLAG = 3, 5, 6
        XS_AT = 3
        NORM_AT = {"narrow": (1, 2, 3, 4), "wide": (3, 4, 4, 5)}
        UPDATE_AT = 6
        SPLITS = {(0, 2): (0, 5),
                  (G - 1, 0): (1, 0), (G - 1, 3): (1, 1), (G - 1, 4): (1, 2), (G - 1, 6): (1, 3),
                  (G - 1, 7): (1, 4), (G, 2): (1, 5),
                  (NARROW_AT - 1, 0): (2, 0), (NARROW_AT - 1, 3): (2, 1), (NARROW_AT - 1, 4): (2, 2),
                  (LAST_AT - 2, 3): (2, 3), (LAST_AT - 1, 1): (2, 4), (LAST_AT, 3): (2, 5)}
        WO_SPLITS = {(t, u): (layer, part) for layer, t in enumerate((0, G, LAST_AT))
                     for part, u in enumerate((2, 4, 6, 7))}
        EARLY = 2 * (G - 3)
        MEAN_AT = {NARROW_AT - 1: 1, NARROW_AT + 1: 4}

        def pieces(u, cur, nxt):
            coming = "first narrow" if cur == "wide" and nxt == "narrow" else nxt
            return ([p for p in PIECES[cur].get(u, ()) if not p[2]] +
                    [p for p in PIECES.get(coming, {}).get(u, ()) if p[2]])

        def chunk(t, c):
            if c < 4:
                return t[:, c * CHUNK:(c + 1) * CHUNK]
            n = KT * INNER // 2
            return t[:, WV0 + (c - 4) * n:WV0 + (c - 3) * n]

        def raw(layer, c):
            if layer == 0 and c == 2:
                return probsT[:, :, :, :].rearrange("p r h t -> p (r h t)")[:, 0:CHUNK]
            turn = (c + (c > 2)) % 2 if layer == 0 else c % 2
            return w_raw[:, turn, 0:CHUNK if c < 4 else KT * INNER // 2]

        def raw_free(layer, c):
            if layer == 0:
                return {3: 1, 4: 2, 5: 4}.get(c, 0)
            return 6 * layer + max(c - 1, 0)

        def step_cols(g):
            return bass.ds(g * GT, GT)

        def walk(eng, step):
            w, n = "wide", "narrow"
            step(0, 0, 0, 0, None, w, w)
            with eng.Fori(1, G - 1) as s:
                step(s, s, s, 0, w, w, w)
            step(G - 1, G - 1, G - 1, 0, w, w, w)
            step(G, G, 0, 1, w, w, w)
            with eng.Fori(G + 1, 2 * G - 1) as s:
                step(s, s, s - G, 1, w, w, w)
            step(2 * G - 1, 2 * G - 1, G - 1, 1, w, w, n)
            step(NARROW_AT, 2 * G, 0, None, w, n, n)
            step(NARROW_AT + 1, 2 * G, 1, None, n, n, n)
            with eng.Fori(1, G // 2 - 1) as i:
                for e in range(2):
                    step(2 * i + (NARROW_AT + e), 2 * G, 2 * i + e, None, n, n, n, e)
            step(LAST_AT - 2, 2 * G, G - 2, None, n, n, n)
            step(LAST_AT - 1, 2 * G, G - 1, None, n, n, w)
            step(LAST_AT, 2 * G, 0, 2, n, w, w)
            step(LAST_AT + 1, 2 * G + 1, 1, 2, w, w, w)
            with eng.Fori(2, G - 1) as g:
                step(g + LAST_AT, g + 2 * G, g, 2, w, w, w)
            step(4 * G - 1, 3 * G - 1, G - 1, 2, w, w, None)

        block = stack.enter_context(nc.Block())

        @block.sync
        def _(sp):
            def load_chunk(layer, c):
                wait(sp, w_hi, raw_free(layer, c))
                wait(sp, w_lo, raw_free(layer, c))
                dst = raw(layer, c)
                if c < 4:
                    cols = slice(256 * c, 256 * c + 256)
                    dst = dst.rearrange("p (m n) -> p m n", m=3)
                    sp.dma_start(dst[:, 0:KT, :],
                                 wk[layer].rearrange("(k p) n -> p k n", p=P)[:, :, cols]).then_inc(w_loaded[c], 16)
                    sp.dma_start(dst[:, KT, :], wq[layer, :, cols]).then_inc(w_loaded[c], 16)
                else:
                    sp.dma_start(dst.rearrange("p (k n) -> p k n", k=KT),
                                 wv[layer].rearrange("(k p) n -> p k n", p=P)[:, :, 512 * (c - 4):512 * (c - 3)])\
                      .then_inc(w_loaded[c], 16)

            def load_wo(layer, part):
                wait(sp, wo_hi, 4 * layer + part - 1)
                wait(sp, wo_lo, 4 * layer + part - 1)
                sp.dma_start(wo_raw[:, part % 2, :, :],
                             wo[layer, 256 * part:256 * part + 256].rearrange("(a p) n -> p a n", p=P))\
                  .then_inc(wo_loaded[part], 16)

            def load_cv(g, b, after):
                if after is not None:
                    wait(sp, after[0], after[1])
                for dst, src in ((cv_h, c_h), (cv_l, c_l)):
                    sp.dma_start(dst[:, b, :, :].bitcast(F32), src[:, :, bass.ds(g * GT + b * T, T)].bitcast(F32))\
                      .then_inc(cv_loaded[b], 16)

            def refresh(layer):
                s = G * layer + G - 1

                def chunk_of_pairs(c):
                    sp.wait_ge(q_ready, 4 * s + c + 1)
                    sp.wait_ge(k_ready, 4 * s + c + 1)
                    load_chunk(layer + 1, c)

                load_cv(G - 1, 0, (v_ready, 4 * s - 1))
                chunk_of_pairs(0)
                load_cv(G - 1, 1, (v_ready, 4 * s))
                for c in range(1, 4):
                    chunk_of_pairs(c)
                load_cv(0, 0, (v_ready, 4 * s + 3))
                load_chunk(layer + 1, 4)
                load_cv(0, 1, (v_ready, 4 * s + 4))
                if layer == 0:
                    load_chunk(layer + 1, 5)
                sp.wait_ge(y_ready, 4 * s + 1)
                load_wo(layer + 1, 0)
                for part in range(1, 4 if layer == 0 else 2):
                    sp.wait_ge(y_ready, 4 * s + part + 1)
                    load_wo(layer + 1, part)

            def load_ctx(part):
                sp.dma_start(ctx_raw[part // 2].rearrange("p (b c) -> p b c", c=CT)
                             [:, 4 * (part % 2):4 * (part % 2) + 4, :],
                             ctx_in[4 * part:4 * part + 4].rearrange("b t c -> t b c"))\
                  .then_inc(ctx_loaded[part], 16)

            def load_x(part):
                sp.dma_start(x_raw.rearrange("p (b c) -> p b c", c=C)[:, 4 * part:4 * part + 4, :],
                             x[4 * part:4 * part + 4].rearrange("b t c -> t b c")).then_inc(x_loaded[part], 16)

            load_ctx(0)
            load_x(0)
            load_chunk(0, 0)
            load_chunk(0, 1)
            load_ctx(1)
            load_ctx(2)
            load_x(1)
            load_chunk(0, 2)
            load_ctx(3)
            load_x(2)
            load_x(3)
            sp.wait_ge(setup_hi, 2)
            sp.wait_ge(setup_lo, 2)
            for b in range(GB):
                load_cv(0, b, None)
            for c in range(3, 5):
                load_chunk(0, c)
            sp.dma_start(bo_sb[:, :], bo).then_inc(columns_loaded, 16)
            sp.dma_start(nw_sb[:, :], norm_w).then_inc(columns_loaded, 16)
            for part in range(2):
                load_wo(0, part)
            sp.wait_ge(setup_t, 12)
            sp.dma_start(nw_raw, nw).then_inc(narrow_loaded, 16)
            sp.dma_start(nwo_raw, nwo).then_inc(narrow_loaded, 16)
            load_chunk(0, 5)
            for part in range(2, 4):
                load_wo(0, part)

            with sp.Fori(1, G - 1) as s:
                for b in range(GB):
                    load_cv(s, b, (v_ready, 4 * s - 1 + b))
            refresh(0)
            with sp.Fori(G + 1, 2 * G - 1) as s:
                for b in range(GB):
                    load_cv(s - G, b, (v_ready, 4 * s - 1 + b))
            refresh(1)
            with sp.Fori(1, G) as g:
                for b in range(GB):
                    load_cv(g, b, (nv_ready, g))
            for b in range(GB):
                load_cv(0, b, (nv_ready, G))
            load_chunk(2, 5)
            for part in range(2, 4):
                load_wo(2, part)

            def store(g):
                wait(sp, fin_copied, g + 1)
                sp.dma_start(out[bass.ds(g * GB, GB)].rearrange("b t c -> t b c"),
                             result_sb[:, step_cols(g)].rearrange("p (b c) -> p b c", b=GB)).then_inc(stored, 16)

            for b in range(GB):
                load_cv(1, b, (v_ready, 8 * G + 3 + b))
            with sp.Fori(2, G) as g:
                for b in range(GB):
                    load_cv(g, b, (v_ready, 4 * g + (8 * G - 1 + b)))
                store(g - 2)
            for g in range(G - 2, G):
                store(g)
            sp.wait_ge(stored, 16 * G)

        @block.gpsimd
        def _(pool):
            pool.memset(ident[:, :], 0.0).then_inc(zeroed, 1)
            pool.wait_ge(zeroed, 1)
            pool.affine_select(out=ident[:, :], in_=ident[:, :], compare_op=ALU.not_equal, fill=1.0, base=0,
                               pattern=[[-1, P]], channel_multiplier=1).then_inc(ident_ready, 1)
            pool.iota(iota_i[:, :], pattern=[[1, T]], base=0, channel_multiplier=0).then_inc(ident_ready, 1)
            pool.memset(ones[:, :], 1.0).then_inc(ident_ready, 1)

            pool.wait_ge(ident_ready, 3)
            cleared = [0]

            def clear(ap):
                cleared[0] += 1
                pool.memset(ap.bitcast(F32), 0.0).then_inc(k_cleared, 1)
                pool.wait_ge(k_cleared, cleared[0])

            for k in (k_h, k_l):
                clear(k[64:128, :, 0, :])
                clear(k[0:64, :, 1, :])

            def norm(n, ring):
                wait(pool, rden_ready, n + 1)
                p = probs[:, ring, :, :]
                pool.tensor_tensor(p, p, rden[:, ring, :].unsqueeze(2).to_broadcast([P, 4, T]), ALU.mult)\
                    .then_inc(norm_done, 1)

            def squares(t, g):
                wait(pool, x_updated, t)
                xg = xT[:, step_cols(g)]
                pool.tensor_tensor(sq[:, step_cols(g)], xg, xg, ALU.mult).then_inc(sq_ready, 1)

            def clear_parity(t, e, after):
                wait(pool, scores_ready, 8 * t + after)
                for k in (k_hf, k_lf):
                    clear(k[:, NK_AT[e]:NK_AT[e] + NK])

            def steps(first, last, with_squares=False):
                with pool.Fori(first, last) as t:
                    for u in range(SLOTS):
                        norm(8 * t + u, u % 4)
                        if with_squares and u == UPDATE_AT + 1:
                            squares(t, t - (G + 1))

            def step_clearing(t, clearing, with_squares):
                for u in range(SLOTS):
                    norm(8 * t + u, u % 4)
                    for at, tt, e, after in clearing:
                        if u == at:
                            clear_parity(tt, e, after)
                    if with_squares and u == UPDATE_AT + 1:
                        squares(t, t - (G + 1))

            steps(0, G + 1)
            steps(G + 1, NARROW_AT - 1, with_squares=True)
            step_clearing(NARROW_AT - 1, [(1, NARROW_AT - 1, 0, 2)], True)
            step_clearing(NARROW_AT, [(0, NARROW_AT, 1, 0)], True)
            steps(NARROW_AT + 1, LAST_AT - 1)
            step_clearing(LAST_AT - 1, [(0, LAST_AT - 1, 0, 0)], False)
            step_clearing(LAST_AT, [(0, LAST_AT, 1, 0)], False)
            steps(LAST_AT + 1, 4 * G)

        @block.tensor
        def _(pe):
            def three(out_ap, lhs, rhs, first, last):
                (a_h, a_l), (b_h, b_l) = lhs, rhs
                pe.matmul(out_ap, a_h, b_l, start=first, stop=False, skip_group_check=True)
                pe.matmul(out_ap, a_l, b_h, start=False, stop=False, skip_group_check=True)
                return pe.matmul(out_ap, a_h, b_h, start=False, stop=last, skip_group_check=True)

            def setup_tile(i):
                what, part = TILES[i][:2]
                pe.wait_ge((ctx_loaded if what == "c" else x_loaded)[part], 16)
                if i >= len(setup_banks):
                    before = i + 1 - len(setup_banks)
                    pe.wait_ge(setup_hi, before)
                    pe.wait_ge(setup_lo, split_by(before))
                for j in range(4):
                    b = 4 * part + j
                    if what == "c":
                        at = (b % 8) * CT + TILES[i][2] * P
                        src = ctx_raw[b // 8][:, at:at + P]
                    else:
                        src = x_raw[:, b * C:(b + 1) * C]
                    mm = pe.transpose(setup_banks[i % len(setup_banks)][:, j * P:(j + 1) * P], src, ident[:, :])
                mm.then_inc(setup_t, 1)

            def weights_wait(chunks):
                pe.wait_ge(w_hi, chunks)
                pe.wait_ge(w_lo, chunks)

            def k_piece(s, g, jj):
                wait(pe, k_hi, 4 * s + jj)
                wait(pe, k_lo, 4 * s + jj)
                for p in range(2):
                    for k in range(KT):
                        at = jj * CHUNK + k * 256 + p * P
                        mm = three(ps_k[:, p * GT:(p + 1) * GT],
                                   (w_h[:, at:at + P], w_l[:, at:at + P]),
                                   (c_h[:, k, step_cols(g)], c_l[:, k, step_cols(g)]), k == 0, k == KT - 1)
                mm.then_inc(k_ready, 1)

            def q_piece(t, s, jj):
                wait(pe, q_hi, 4 * s + jj)
                wait(pe, q_lo, 4 * s + jj)
                wait(pe, xs_hi, t + 1)
                wait(pe, xs_lo, t + 1)
                for p in range(2):
                    at = jj * CHUNK + 2 * 256 + p * P
                    mm = three(ps_q[:, p * GT:(p + 1) * GT], (w_h[:, at:at + P], w_l[:, at:at + P]),
                               (xs_h[:, :], xs_l[:, :]), True, True)
                mm.then_inc(q_ready, 1)

            def v_piece(t, s, i):
                b, half = i % 2, i // 2
                wait(pe, v_copied, 4 * s + i)
                wait(pe, cv_loaded[b], 32 * (t + 1))
                for k in range(KT):
                    at = WV0 + half * KT * 512 + k * 512
                    mm = three(ps_v[:, :], (cv_h[:, b, k, :], cv_l[:, b, k, :]),
                               (w_h[:, at:at + 512], w_l[:, at:at + 512]), k == 0, k == KT - 1)
                mm.then_inc(v_ready, 1)

            def nk_piece(g):
                wait(pe, nk_hi, g)
                wait(pe, nk_lo, g)
                dst = ps_k[:, 0:GT]
                for k in range(KT):
                    mm = three(dst, (nw_h[:, 4 + k, :], nw_l[:, 4 + k, :]),
                               (c_h[:, k, step_cols(g)], c_l[:, k, step_cols(g)]), k == 0, k == KT - 1)
                mm.then_inc(nk_ready, 1)

            def nq_piece(t, g, half):
                wait(pe, nq_hi, 2 * g + half)
                wait(pe, nq_lo, 2 * g + half)
                wait(pe, xs_hi, t + 1)
                wait(pe, xs_lo, t + 1)
                for i in range(2):
                    r = 2 * half + i
                    mm = three(ps_q[:, i * GT:(i + 1) * GT], (nw_h[:, r, :], nw_l[:, r, :]),
                               (xs_h[:, :], xs_l[:, :]), True, True)
                mm.then_inc(nq_ready, 1)

            def nv_piece(t, g):
                wait(pe, nv_copied, g)
                for b in range(GB):
                    wait(pe, cv_loaded[b], 32 * (t + 1))
                    for k in range(KT):
                        mm = three(ps_v[:, b * P:(b + 1) * P], (cv_h[:, b, k, :], cv_l[:, b, k, :]),
                                   (nw_h[:, 6 + k, :], nw_l[:, 6 + k, :]), k == 0, k == KT - 1)
                mm.then_inc(nv_ready, 1)

            def scores_wide(n, s, u):
                jj, b = u // 2, u % 2
                wait(pe, exp_done, n - 1)
                if b == 0:
                    for part in (k_hi, k_lo, q_hi, q_lo):
                        wait(pe, part, 4 * s + jj + 1)
                for p in range(2):
                    pair, tok = 2 * jj + p, slice(b * T, (b + 1) * T)
                    mm = three(ps_s[u % 2][:, p * 2 * T:(p + 1) * 2 * T].rearrange("p (h t) -> p h t", h=2),
                               (q_h[:, pair, tok], q_l[:, pair, tok]),
                               (k_h[:, pair, :, tok], k_l[:, pair, :, tok]), True, True)
                mm.then_inc(scores_ready, 1)

            def scores_narrow(n, g, e, u):
                r, b = u // 2, u % 2
                wait(pe, exp_done, n - 1)
                if u == 0:
                    wait(pe, nk_hi, g + 1)
                    wait(pe, nk_lo, g + 1)
                if u in (0, 4):
                    wait(pe, nq_hi, 2 * g + u // 4 + 1)
                    wait(pe, nq_lo, 2 * g + u // 4 + 1)
                tok = slice(b * T, (b + 1) * T)
                three(ps_s[u % 2][:, :].rearrange("p (h t) -> p h t", h=4),
                      (nq_h[e][:, r, tok], nq_l[e][:, r, tok]),
                      (nk_h[e][:, :, tok], nk_l[e][:, :, tok]), True, True).then_inc(scores_ready, 1)

            def transposes(n, u):
                wait(pe, norm_done, n + 1)
                wait(pe, pt_copied, n)
                for h in range(4):
                    mm = pe.transpose(ps_t[:, h * T:(h + 1) * T], probs[:, u % 4, h, :], ident[:, :])
                mm.then_inc(pt_ready, 1)

            def weigh(k, jj, kind, e, v_count):
                wait(pe, pt_copied, 2 * k + 2)
                wait(pe, o_hi, k)
                wait(pe, o_lo, k)
                wait(pe, v_copied if kind == "wide" else nv_copied, v_count)
                for b in range(GB):
                    for h in range(4):
                        if kind == "wide":
                            half, p = h % 2, h // 2
                            at = (4 * jj + h) * HD
                            mm = pe.matmul(ps_o[half * HD:(half + 1) * HD, p * GT + b * T:p * GT + (b + 1) * T],
                                           v_sb[:, b, at:at + HD], probsT[:, b, h, :], start=True, stop=True)
                        else:
                            mm = pe.matmul(ps_o[32 * h:32 * h + 32, b * T:(b + 1) * T],
                                           nv[e][:, b, 32 * h:32 * h + 32], probsT[:, b, h, :], start=True,
                                           stop=True)
                mm.then_inc(o_ready, 1)

            def y_piece(t, jj, kind, n_wo):
                wait(pe, o_hi, 4 * t + jj + 1)
                wait(pe, o_lo, 4 * t + jj + 1)
                if jj == 0:
                    wait(pe, x_updated, t)
                if kind == "wide":
                    pe.wait_ge(wo_hi, n_wo)
                    pe.wait_ge(wo_lo, n_wo)
                    for a in range(2):
                        mm = three(ps_y[:, 0:GT], (wo_h[:, 2 * jj + a, :], wo_l[:, 2 * jj + a, :]),
                                   (o_h[:, jj % 2, a, :], o_l[:, jj % 2, a, :]), jj + a == 0, jj + a == 4)
                else:
                    mm = three(ps_y[:, 0:GT], (nwo_h[:, jj, :], nwo_l[:, jj, :]),
                               (o_h[:, jj % 2, 0, :], o_l[:, jj % 2, 0, :]), jj == 0, jj == 3)
                mm.then_inc(y_ready, 1)

            def means(first, last):
                pe.wait_ge(sq_ready, (last + 1) // GB)
                for b in range(first, last):
                    mm = pe.matmul(ps_v[:, b:b + 1], sq[:, b * T:(b + 1) * T], ones[:, 0:1], start=True,
                                   stop=True)
                mm.then_inc(mean_ready, 1)

            def spread(g):
                wait(pe, diag_ready, g + 1)
                pe.matmul(ps_q[:, 0:GT], ones[:, :], diag.rearrange("p b t -> p (b t)"), start=True, stop=True)\
                  .then_inc(spread_ready, 1)

            def result(g):
                wait(pe, x_updated, g + (LAST_AT + 1))
                for b in range(GB):
                    mm = pe.transpose(ps_v[:, b * P:(b + 1) * P], last_x[:, b * T:(b + 1) * T], ident[:, :])
                mm.then_inc(fin_t, 1)

            def step(t, s, g, layer, prv, cur, nxt, e=None):
                first = isinstance(s, int) and isinstance(g, int) and g == 0
                last = isinstance(g, int) and g == G - 1
                if e is None and cur == "narrow":
                    e = g % 2
                s_next = s + (cur == "wide")
                g_next = 0 if last else g + 1
                for u in range(SLOTS):
                    n = 8 * t + u
                    if cur == "wide":
                        scores_wide(n, s, u)
                    else:
                        scores_narrow(n, g, e, u)
                    if u % 2 and not (prv is None and u < PLAG):
                        jj = (u - PLAG) // 2
                        kind = cur if jj >= 0 else prv
                        if kind == "wide":
                            count = 4 * s + (2 * (jj // 2) + 2 if jj >= 0 else 0)
                        else:
                            count = g + 1 if jj >= 0 else (G if cur == "wide" else g)
                        weigh(4 * t + jj, jj % 4, kind, e if jj >= 0 else (1 if cur == "wide" else 1 - (e or 0)),
                              count)
                    if not (prv is None and u < TLAG):
                        transposes(n - TLAG, (u - TLAG) % 8)
                    for what, i, ahead in pieces(u, cur, nxt):
                        if what == "k":
                            if first and not ahead:
                                weights_wait(6 * layer + i + 1)
                            elif ahead and last:
                                weights_wait(6 * (layer + 1 if cur == "wide" else 2) + i + 1)
                            if cur == "narrow" and i == 0:
                                pe.wait_ge(nk_hi, G)
                                pe.wait_ge(nk_lo, G)
                            k_piece(s_next if ahead else s, g_next if ahead else g, i)
                        elif what == "q":
                            if first and not ahead:
                                weights_wait(6 * layer + i + 1)
                            elif ahead and last:
                                weights_wait(6 * (layer + 1 if cur == "wide" else 2) + i + 1)
                            if cur == "narrow" and i == 0:
                                pe.wait_ge(nq_hi, 2 * G)
                                pe.wait_ge(nq_lo, 2 * G)
                            q_piece(t + ahead, s_next if ahead else s, i)
                        elif what == "v":
                            if first:
                                weights_wait(6 * layer + 5 + i // 2)
                            if i == 0 and prv == "narrow":
                                pe.wait_ge(nv_copied, G)
                            if i == 0 and layer == 2 and not (isinstance(g, int) and g < 2):
                                wait(pe, fin_copied, g - 1)
                            if i == 1 and isinstance(t, int) and t == NARROW_AT - 1:
                                pe.wait_ge(mean_copied, 1)
                            v_piece(t, s, i)
                        elif what == "nk":
                            if cur == "wide":
                                pe.wait_ge(k_hi, 8 * G)
                                pe.wait_ge(k_lo, 8 * G)
                                pe.wait_ge(nw_hi, 2)
                                pe.wait_ge(nw_lo, 2)
                            nk_piece(g_next)
                        elif what == "nq":
                            nq_piece(t + ahead, g_next if ahead else g, i)
                        elif what == "nv":
                            if first:
                                pe.wait_ge(v_copied, 8 * G)
                            elif not isinstance(t, int) or t > NARROW_AT + 1:
                                pe.wait_ge(mean_copied, 2)
                            nv_piece(t, g)
                    if nxt == "narrow" and u == NORM_AT[cur][1]:
                        for part in ((q_hi, q_lo) if cur == "wide" else (nq_hi, nq_lo)):
                            wait(pe, part, 8 * G if cur == "wide" else 2 * g + 2)
                        spread(g_next)
                    if isinstance(t, int) and u == MEAN_AT.get(t):
                        if cur == "wide":
                            pe.wait_ge(v_copied, 4 * s + 1)
                            means(0, EARLY)
                        else:
                            pe.wait_ge(nv_copied, g + 1)
                            means(EARLY, B)
                    if u % 2 and (u == 7 or prv):
                        jj = (u // 2 + 1) % 4
                        if u == 7:
                            y_piece(t, 0, cur, None if layer is None else 4 * layer + 1 if first
                                    else 4 * layer + 4)
                        else:
                            y_piece(t - 1, jj, prv, 4 * (layer + 1) if layer is not None and not first
                                    else 4 * layer if layer is not None and prv == "wide" else 8)
                    if layer == 2 and u == UPDATE_AT + 1 and not first:
                        wait(pe, v_copied, 4 * s + 4)
                        result(g - 1)

            pe.wait_ge(ident_ready, 1)
            for item in SETUP:
                if item[0] in ("c", "x"):
                    setup_tile(TILES.index(item))
                elif item[0] == "bias":
                    pe.wait_ge(rows_ready, WIDE)
                    pe.matmul(ps_t[:, 0:WIDE * T], alpha[:, :], sel[:, :, :].rearrange("p l t -> p (l t)"),
                              start=True, stop=True).then_inc(bias_made, 1)
                elif item[0] in ("k", "q"):
                    if item == ("k", 0):
                        pe.wait_ge(setup_hi, 2)
                        pe.wait_ge(setup_lo, 2)
                    weights_wait(item[1] + 1)
                    if item[0] == "k":
                        k_piece(0, 0, item[1])
                    else:
                        q_piece(0, 0, item[1])
            pe.wait_ge(setup_hi, 12)
            pe.wait_ge(setup_lo, 8)
            pe.wait_ge(k_cleared, 4)
            pe.wait_ge(bias_ready, 1)
            walk(pe, step)
            t = 4 * G
            transposes(8 * t - 3, 5)
            weigh(4 * t - 2, 2, "wide", None, 12 * G)
            transposes(8 * t - 2, 6)
            y_piece(t - 1, 1, "wide", 12)
            transposes(8 * t - 1, 7)
            weigh(4 * t - 1, 3, "wide", None, 12 * G)
            y_piece(t - 1, 2, "wide", 12)
            y_piece(t - 1, 3, "wide", 12)
            pe.wait_ge(fin_copied, G - 1)
            result(G - 1)

        @block.scalar
        def _(act):
            act.dma_start(rows_sb[:, :], rows).then_inc(small_loaded, 16)
            act.dma_start(tok_i[:, :], tokens).then_inc(small_loaded, 16)

            def setup_tile(i):
                act.wait_ge(setup_t, i + 1)
                what, part = TILES[i][:2]
                cols = slice(512 * part, 512 * part + 512)
                dst = c_h[:, TILES[i][2], cols] if what == "c" else xT[:, cols]
                act.activation(dst, setup_banks[i % len(setup_banks)][:, :], ACT.Copy).then_inc(setup_hi, 1)

            def split(layer, c):
                act.wait_ge(w_loaded[c], (32 if c < 4 else 16) * (layer + 1))
                act.activation(chunk(w_h, c), raw(layer, c), ACT.Copy).then_inc(w_hi, 1)

            def split_wo(layer, part):
                act.wait_ge(wo_loaded[part], 16 * (layer + 1))
                a = slice(2 * part, 2 * part + 2)
                act.activation(wo_h[:, a, :], wo_raw[:, part % 2, :, :], ACT.Copy).then_inc(wo_hi, 1)

            def split_narrow():
                act.wait_ge(columns_loaded, 16 * 2)
                act.wait_ge(narrow_loaded, 16 * 2)
                act.activation(nw_h[:, :, :], nw_raw, ACT.Copy).then_inc(nw_hi, 1)
                act.activation(nwo_h[:, :, :], nwo_raw, ACT.Copy).then_inc(nw_hi, 1)

            def split_x(g, kind, after, used):
                if kind == "wide":
                    wait(act, x_updated, after)
                else:
                    wait(act, xn_ready, g + 1)
                if used is not None:
                    wait(act, used[0], used[1])
                if kind == "wide":
                    act.activation(xs_h[:, :], xT[:, step_cols(g)], ACT.Copy).then_inc(xs_hi, 1)
                else:
                    act.activation(xs_h[:, :], xn[:, :], ACT.Copy).then_inc(xs_hi, 1)

            def k_upper(s, jj):
                wait(act, k_ready, 4 * s + jj + 1)
                src = ps_k[:, :].rearrange("p (a t) -> p a t", a=2)
                for half in range(2):
                    rows = slice(64 * half, 64 * half + 64)
                    last = act.activation(k_h[rows, 2 * jj:2 * jj + 2, half, :], src[rows], ACT.Copy)
                last.then_inc(k_hi, 1)

            def q_upper(s, jj):
                wait(act, q_ready, 4 * s + jj + 1)
                act.activation(q_h[:, 2 * jj:2 * jj + 2, :], ps_q[:, :].rearrange("p (a t) -> p a t", a=2),
                               ACT.Copy, scale=-HD ** -0.5).then_inc(q_hi, 1)

            def v_copy(s, i):
                wait(act, v_ready, 4 * s + i + 1)
                act.activation(v_sb[:, i % 2, 512 * (i // 2):512 * (i // 2) + 512], ps_v[:, :], ACT.Copy)\
                   .then_inc(v_copied, 1)

            def nk_upper(g, e):
                wait(act, nk_ready, g + 1)
                for h in range(KV):
                    rows = slice(32 * h, 32 * h + 32)
                    last = act.activation(nk_h[e][rows, h, :], ps_k[rows, 0:GT], ACT.Copy)
                last.then_inc(nk_hi, 1)

            def nq_upper(g, e, half):
                wait(act, nq_ready, 2 * g + half + 1)
                act.activation(nq_h[e][:, 2 * half:2 * half + 2, :],
                               ps_q[:, :].rearrange("p (a t) -> p a t", a=2), ACT.Copy,
                               scale=RD ** -0.5).then_inc(nq_hi, 1)

            def nv_copy(g, e):
                wait(act, nv_ready, g + 1)
                if isinstance(g, int) and g == 0:
                    act.wait_ge(o_ready, 4 * NARROW_AT)
                act.activation(nv[e], ps_v[:, 0:GB * P].rearrange("p (b n) -> p b n", b=GB), ACT.Copy)\
                   .then_inc(nv_copied, 1)

            def roots(first, last, count):
                act.wait_ge(mean_copied, count)
                act.activation(root[:, first:last], root[:, first:last], ACT.Sqrt, bias=eps_sb[:, :],
                               scale=1.0 / C).then_inc(root_ready, 1)

            def result_copy(g):
                wait(act, fin_t, g + 1)
                act.activation(result_sb[:, step_cols(g)], ps_v[:, 0:GB * C], ACT.Copy).then_inc(fin_copied, 1)

            def exps(n, u, kind):
                wait(act, max_ready, n + 1)
                wait(act, pt_ready, n - 3)
                scale = -1.0 if kind == "wide" else 1.0
                for h in range(4):
                    last = act.activation(probs[:, u % 4, h, :], ps_s[u % 2][:, h * T:(h + 1) * T], ACT.Exp,
                                          scale=scale, bias=nmax[:, u % 4, h:h + 1],
                                          accum_out=den[:, u % 4, h:h + 1])
                last.then_inc(exp_done, 1)

            def o_upper(k, jj, kind):
                wait(act, o_ready, k + 1)
                wait(act, y_ready, k - 1)
                if kind == "wide":
                    act.activation(o_h[:, jj % 2, :, :], ps_o[:, :].rearrange("p (a t) -> p a t", a=2), ACT.Copy)\
                       .then_inc(o_hi, 1)
                else:
                    act.activation(o_h[:, jj % 2, 0, :], ps_o[:, 0:GT], ACT.Copy).then_inc(o_hi, 1)

            def upper(s, s_next, g_next, e_next, g, e, found, clears):
                for what, i, ahead in found:
                    if what in clears and i == clears[what][0]:
                        act.wait_ge(k_cleared, clears[what][1])
                    if what == "k":
                        k_upper(s_next if ahead else s, i)
                    elif what == "q":
                        q_upper(s_next if ahead else s, i)
                    elif what == "v":
                        v_copy(s, i)
                    elif what == "nk":
                        nk_upper(g_next, e_next)
                    elif what == "nq":
                        nq_upper(g_next if ahead else g, e_next if ahead else e, i)
                    elif what == "nv":
                        nv_copy(g, e)

            def step(t, s, g, layer, prv, cur, nxt, e=None):
                last = isinstance(g, int) and g == G - 1
                known = isinstance(t, int)
                if e is None:
                    e = g % 2 if cur == "narrow" else 1
                s_next = s + (cur == "wide")
                g_next = 0 if last else g + 1
                e_next = 0 if cur == "wide" else 1 - e
                clears = {NARROW_AT - 1: {"nk": (0, 6)}, NARROW_AT: {"nk": (0, 8)}, LAST_AT - 1: {"k": (0, 10)},
                          LAST_AT: {"k": (3, 12)}}.get(t, {}) if known else {}
                for u in range(SLOTS):
                    n, jj = 8 * t + u, (u - OLAG) // 2
                    if u % 2 == 0 and not (prv is None and jj < 0):
                        o_upper(4 * t + jj, jj % 4, cur if jj >= 0 else prv)
                    if layer == 2 and u == 0 and not (known and g < 2):
                        result_copy(g - 2)
                    if u:
                        upper(s, s_next, g_next, e_next, g, e, pieces(u - 1, cur, nxt), clears)
                    elif prv:
                        upper(s - 1, s, g, e, g, e, pieces(7, prv, cur), {})
                    if known and (t, u) in SPLITS:
                        split(*SPLITS[t, u])
                    if known and (t, u) in WO_SPLITS:
                        split_wo(*WO_SPLITS[t, u])
                    if known and (t, u) == (0, SLOTS - 1):
                        split_narrow()
                    if nxt and u == (NORM_AT[cur][3] if nxt == "narrow" else XS_AT):
                        if cur == "wide":
                            used = (q_ready, 4 * s + 4)
                        else:
                            used = (nq_ready, 2 * g + 2)
                        split_x(g_next, nxt, 0 if layer == 0 and not last else t - 6, used)
                    if known and t == NARROW_AT - 1 and u == MEAN_AT[t] + 1:
                        roots(0, EARLY, 1)
                    if known and t == NARROW_AT + 1 and u == MEAN_AT[t] + 1:
                        roots(EARLY, B, 2)
                    exps(n, u, cur)

            for item in SETUP:
                if item[0] in ("c", "x"):
                    setup_tile(TILES.index(item))
                elif item[0] == "w":
                    split(0, item[1])
                elif item[0] == "xs":
                    act.wait_ge(setup_hi, TILES.index(("x", 0)) + 1)
                    split_x(0, "wide", 0, None)
                elif item[0] in ("k", "q"):
                    (k_upper if item[0] == "k" else q_upper)(0, item[1])
            act.wait_ge(setup_hi, 12)
            walk(act, step)
            result_copy(G - 2)
            for jj in range(1, 4):
                o_upper(16 * G - 4 + jj, jj, "wide")
            result_copy(G - 1)

        @block.vector
        def _(dve):
            dve.memset(eps_sb[:, :], EPS)
            done = [0]

            def then(ins):
                done[0] += 1
                ins.then_inc(rows_step, 1)
                dve.wait_ge(rows_step, done[0])

            then(dve.memset(sel[:, :, :].bitcast(F32), 0.0))

            mask, flags = rows_sb[:, 0:T], rows_sb[:, T:T + 4]

            def find_tokens(k, dst):
                hit = ps_t[0:ROWS, :].rearrange("p (j t) -> p j t", j=4)
                then(dve.tensor_tensor(hit, iota_f[:, :].unsqueeze(1).to_broadcast([ROWS, 4, T]),
                                       tok_f[:, k, :].unsqueeze(2).to_broadcast([ROWS, 4, T]), ALU.is_equal))
                then(dve.tensor_reduce(dst, hit.rearrange("p j t -> p t j"), AX.X, ALU.max))

            def make_rows(half):
                if half == 0:
                    dve.wait_ge(small_loaded, 16 * 2)
                    then(dve.tensor_scalar(mask, mask, -1.0, 1.0, ALU.mult, ALU.add))
                    then(dve.tensor_scalar(mask, mask, SUPPRESS, None, ALU.mult))
                    then(dve.tensor_copy(alpha[:, :], mask))
                    then(dve.tensor_tensor(mask, mask, alpha[:, :].bitcast(F32), ALU.subtract))
                    then(dve.tensor_scalar(mask, mask, flags[:, 2:3], None, ALU.mult))
                    then(dve.scalar_tensor_tensor(out=alpha[:, :], in0=alpha[:, :].bitcast(F32),
                                                  scalar=flags[:, 1:2], in1=mask, op0=ALU.mult, op1=ALU.add))
                    then(dve.tensor_copy(tok_f[:, :, 0:2], tok_i[:, :].rearrange("p (k c) -> p k c", k=2)))
                    then(dve.tensor_scalar(tok_f[:, :, 2:4], tok_f[:, :, 0:2], float(T), None, ALU.add))
                    dve.wait_ge(ident_ready, 2)
                    then(dve.tensor_copy(iota_f[:, :], iota_i[:, :]))
                    find_tokens(0, own)
                    return
                find_tokens(1, of_b)
                then(dve.scalar_tensor_tensor(out=of_b, in0=of_b, scalar=flags[:, 0:1], in1=own, op0=ALU.mult,
                                              op1=ALU.mult))
                for layer in range(WIDE):
                    of = slice(32 * layer, 32 * layer + 32)
                    dve.tensor_tensor(sel[of, layer, :], own[of], of_b[of], ALU.subtract).then_inc(rows_ready, 1)

            def setup_tile(i):
                if TILES[i][0] == "c":
                    _, part, k = TILES[i]
                    dve.wait_ge(setup_hi, i + 1)
                    cols = slice(512 * part, 512 * part + 512)
                    dve.tensor_tensor(c_l[:, k, cols], setup_banks[i % len(setup_banks)][:, :],
                                      c_h[:, k, cols].bitcast(F32), ALU.subtract).then_inc(setup_lo, 1)

            def split(layer, c):
                dve.wait_ge(w_hi, 6 * layer + c + 1)
                dve.tensor_tensor(chunk(w_l, c), raw(layer, c), chunk(w_h, c).bitcast(F32),
                                  ALU.subtract).then_inc(w_lo, 1)

            def split_wo(layer, part):
                dve.wait_ge(wo_hi, 4 * layer + part + 1)
                a = slice(2 * part, 2 * part + 2)
                dve.tensor_tensor(wo_l[:, a, :], wo_raw[:, part % 2, :, :], wo_h[:, a, :].bitcast(F32),
                                  ALU.subtract).then_inc(wo_lo, 1)

            def split_narrow():
                for i, (came, high, low) in enumerate(((nw_raw, nw_h, nw_l), (nwo_raw, nwo_h, nwo_l))):
                    dve.wait_ge(nw_hi, i + 1)
                    dve.tensor_tensor(low[:, :, :], came, high[:, :, :].bitcast(F32), ALU.subtract)\
                       .then_inc(nw_lo, 1)

            def split_x(t, g, kind):
                wait(dve, xs_hi, t + 1)
                if kind == "wide":
                    dve.tensor_tensor(xs_l[:, :], xT[:, step_cols(g)], xs_h[:, :].bitcast(F32), ALU.subtract)\
                       .then_inc(xs_lo, 1)
                else:
                    dve.tensor_tensor(xs_l[:, :], xn[:, :], xs_h[:, :].bitcast(F32), ALU.subtract)\
                       .then_inc(xs_lo, 1)

            def copy_means(first, last, count):
                dve.wait_ge(mean_ready, count)
                dve.tensor_copy(root[:, first:last], ps_v[:, first:last]).then_inc(mean_copied, 1)

            def diagonals(g):
                dve.wait_ge(root_ready, 1 if isinstance(g, int) and g < EARLY // GB else 2)
                dve.reciprocal(inv[:, :], root[:, bass.ds(g * GB, GB)]).then_inc(inv_ready, 1)
                wait(dve, inv_ready, g + 1)
                for b in range(GB):
                    last = dve.tensor_scalar(diag[:, b, :], ident[:, :], inv[:, b:b + 1], None, ALU.mult)
                last.then_inc(diag_ready, 1)

            def normalise(g):
                wait(dve, spread_ready, g + 1)
                dve.scalar_tensor_tensor(out=xn[:, :], in0=xT[:, step_cols(g)], scalar=nw_sb[:, 0:1],
                                         in1=ps_q[:, 0:GT], op0=ALU.mult, op1=ALU.mult).then_inc(xn_ready, 1)

            def k_lower(s, jj):
                wait(dve, k_hi, 4 * s + jj + 1)
                src = ps_k[:, :].rearrange("p (a t) -> p a t", a=2)
                for half in range(2):
                    rows = slice(64 * half, 64 * half + 64)
                    pair = slice(2 * jj, 2 * jj + 2)
                    last = dve.tensor_tensor(k_l[rows, pair, half, :], src[rows],
                                             k_h[rows, pair, half, :].bitcast(F32), ALU.subtract)
                last.then_inc(k_lo, 1)

            def q_lower(s, jj):
                wait(dve, q_hi, 4 * s + jj + 1)
                pair = slice(2 * jj, 2 * jj + 2)
                dve.scalar_tensor_tensor(out=q_l[:, pair, :], in0=ps_q[:, :].rearrange("p (a t) -> p a t", a=2),
                                         scalar=-HD ** -0.5, in1=q_h[:, pair, :].bitcast(F32), op0=ALU.mult,
                                         op1=ALU.subtract).then_inc(q_lo, 1)

            def nk_lower(g, e):
                wait(dve, nk_hi, g + 1)
                for h in range(KV):
                    rows = slice(32 * h, 32 * h + 32)
                    last = dve.tensor_tensor(nk_l[e][rows, h, :], ps_k[rows, 0:GT],
                                             nk_h[e][rows, h, :].bitcast(F32), ALU.subtract)
                last.then_inc(nk_lo, 1)

            def nq_lower(g, e, half):
                wait(dve, nq_hi, 2 * g + half + 1)
                r = slice(2 * half, 2 * half + 2)
                dve.scalar_tensor_tensor(out=nq_l[e][:, r, :], in0=ps_q[:, :].rearrange("p (a t) -> p a t", a=2),
                                         scalar=RD ** -0.5, in1=nq_h[e][:, r, :].bitcast(F32), op0=ALU.mult,
                                         op1=ALU.subtract).then_inc(nq_lo, 1)

            def update_x(t, g, layer):
                wait(dve, y_ready, 4 * t + 4)
                xg = xT[:, step_cols(g)]
                if layer is None:
                    dve.tensor_tensor(xg, ps_y[:, 0:GT], xg, ALU.add).then_inc(x_updated, 1)
                else:
                    dve.scalar_tensor_tensor(out=xg if layer < 2 else last_x[:, :], in0=ps_y[:, 0:GT],
                                             scalar=bo_sb[:, layer:layer + 1], in1=xg, op0=ALU.add,
                                             op1=ALU.add).then_inc(x_updated, 1)

            def minima(n, u, layer):
                wait(dve, scores_ready, n + 1)
                dve.memset(gate[:, :], 0.0)
                for h in range(4):
                    sc = ps_s[u % 2][:, h * T:(h + 1) * T]
                    last = dve.tensor_tensor_reduce(sc, sc, bias[:, layer, :], 1.0, FAR, ALU.add, ALU.min,
                                                    nmax[:, u % 4, h:h + 1])
                last.then_inc(max_ready, 1)

            def maxima(n, u):
                wait(dve, scores_ready, n + 1)
                dve.tensor_reduce(nmax[:, u % 4, :], ps_s[u % 2][:, :].rearrange("p (h t) -> p h t", h=4),
                                  AX.X, ALU.max, negate=True).then_inc(max_ready, 1)

            def sums(n, u):
                wait(dve, exp_done, n + 1)
                dve.reciprocal(rden[:, u % 4, :], den[:, u % 4, :]).then_inc(rden_ready, 1)

            def pt_copy(n, u, weighed):
                wait(dve, pt_ready, n + 1)
                wait(dve, o_ready, weighed)
                dve.tensor_copy(probsT[:, u % 2, :, :], ps_t[:, :].rearrange("p (h t) -> p h t", h=4))\
                   .then_inc(pt_copied, 1)

            def o_lower(k, jj, kind):
                wait(dve, o_hi, k + 1)
                if kind == "wide":
                    dve.tensor_tensor(o_l[:, jj % 2, :, :], ps_o[:, :].rearrange("p (a t) -> p a t", a=2),
                                      o_h[:, jj % 2, :, :].bitcast(F32), ALU.subtract).then_inc(o_lo, 1)
                else:
                    dve.tensor_tensor(o_l[:, jj % 2, 0, :], ps_o[:, 0:GT], o_h[:, jj % 2, 0, :].bitcast(F32),
                                      ALU.subtract).then_inc(o_lo, 1)

            def lower(s, s_next, g_next, e_next, g, e, found):
                for what, i, ahead in found:
                    if what == "k":
                        k_lower(s_next if ahead else s, i)
                    elif what == "q":
                        q_lower(s_next if ahead else s, i)
                    elif what == "nk":
                        nk_lower(g_next, e_next)
                    elif what == "nq":
                        nq_lower(g_next if ahead else g, e_next if ahead else e, i)

            def step(t, s, g, layer, prv, cur, nxt, e=None):
                first = isinstance(g, int) and g == 0
                last = isinstance(g, int) and g == G - 1
                known = isinstance(t, int)
                if e is None:
                    e = g % 2 if cur == "narrow" else 1
                s_next = s + (cur == "wide")
                g_next = 0 if last else g + 1
                e_next = 0 if cur == "wide" else 1 - e
                for u in range(SLOTS):
                    n = 8 * t + u
                    if known and t in MEAN_AT and u == MEAN_AT[t] + 1:
                        copy_means(*((0, EARLY, 1) if cur == "wide" else (EARLY, B, 2)))
                    if cur == "wide":
                        if not (prv is None and u < 1):
                            sums(n - 1, (u - 1) % 8)
                        minima(n, u, layer)
                    else:
                        maxima(n, u)
                        sums(n - 1, (u - 1) % 8)
                    jj = (u - OLAG) // 2
                    if u % 2 == 0 and not (prv is None and jj < 0):
                        o_lower(4 * t + jj, jj % 4, cur if jj >= 0 else prv)
                    if not (prv is None and u < TLAG):
                        pt_copy(n - TLAG, (u - TLAG) % 8, 4 * t + (u - TLAG) // 2)
                    if u == UPDATE_AT and prv:
                        update_x(t - 1, G - 1 if first else g - 1,
                                 (layer if not first else layer - 1) if layer is not None and prv == "wide"
                                 else 1 if prv == "wide" else None)
                    if u:
                        lower(s, s_next, g_next, e_next, g, e, pieces(u - 1, cur, nxt))
                    elif prv:
                        lower(s - 1, s, g, e, g, e, pieces(7, prv, cur))
                    if known and (t, u) in SPLITS:
                        split(*SPLITS[t, u])
                    if known and (t, u) in WO_SPLITS:
                        split_wo(*WO_SPLITS[t, u])
                    if known and (t, u) == (0, SLOTS - 1):
                        split_narrow()
                    if nxt == "narrow" and u == NORM_AT[cur][0]:
                        diagonals(g_next)
                    if nxt == "narrow" and u == NORM_AT[cur][2]:
                        normalise(g_next)
                    if nxt and u == (NORM_AT[cur][3] if nxt == "narrow" else XS_AT):
                        split_x(t + 1, g_next, nxt)

            for item in SETUP:
                if item[0] in ("c", "x"):
                    setup_tile(TILES.index(item))
                elif item[0] == "w":
                    split(0, item[1])
                elif item[0] == "xs":
                    split_x(0, 0, "wide")
                elif item[0] == "rows":
                    make_rows(item[1])
                elif item[0] == "bias":
                    dve.wait_ge(bias_made, 1)
                    dve.tensor_copy(bias[:, :, :].rearrange("p l t -> p (l t)"), ps_t[:, 0:WIDE * T])\
                       .then_inc(bias_ready, 1)
                else:
                    (k_lower if item[0] == "k" else q_lower)(0, item[1])
            dve.wait_ge(setup_hi, 12)
            dve.wait_ge(columns_loaded, 16 * 2)
            walk(dve, step)
            sums(32 * G - 1, 7)
            for m in range(-TLAG, 0):
                if m != -2:
                    o_lower(16 * G + (m - 3) // 2, (m - 3) // 2 + 4, "wide")
                pt_copy(32 * G + m, m + 8, (32 * G + m) // 2)
            o_lower(16 * G - 1, 3, "wide")
            update_x(4 * G - 1, G - 1, 2)


def kernel(**inputs):
    import numpy as _np
    import concourse.bacc as _bacc
    from concourse import mybir as _mybir
    from concourse.bass_utils import run_bass_kernel_spmd as _run

    a = {k: _np.asarray(v) for k, v in inputs.items()}
    wide = ("L0", "L1", "L3")

    def stacked(name):
        return _np.stack([a[f"{w}_xattn_{name}"] for w in wide])

    masks = (a["mask_S_fk1"], a["mask_S_fk0"])
    tokens = [stacked("token_indices_A"), stacked("token_indices_B")]
    rows = _np.zeros((ROWS, T + 4), masks[0].dtype)
    row_tokens = _np.zeros((ROWS, 4), tokens[0].dtype)
    for layer in range(WIDE):
        for j in range(4):
            r = 32 * layer + j
            rows[r, :T] = masks[j % 2]
            rows[r, T:T + 3] = (j % 2 == 0, j < 2, j >= 2)
            row_tokens[r, 0:2], row_tokens[r, 2:4] = tokens[j % 2][layer], tokens[1][layer]

    def spread(w):
        out = _np.zeros((w.shape[0], KV, P // KV), w.dtype)
        out[:, :, :RD] = w.reshape(w.shape[0], KV, RD)
        return out.reshape(w.shape[0], P)

    nwq = a["L2_xattn_wq"].reshape(C, KV, REP, RD)
    nwo = a["L2_xattn_wo"].reshape(KV, REP, RD, C)
    nw = _np.stack([spread(nwq[:, :, r].reshape(C, KV * RD)) for r in range(REP)] +
                   [spread(a[f"L2_xattn_{name}"][k * P:(k + 1) * P]) for name in ("wk", "wv") for k in range(KT)],
                   axis=1)
    nwo = _np.stack([spread(nwo[:, r].reshape(KV * RD, C).T).T for r in range(REP)], axis=1)
    arrays = {
        "x": a["x"], "ctx_in": a["ctx_2048"], "rows": rows, "tokens": row_tokens, "wq": stacked("Wq"),
        "wk": stacked("Wk"), "wv": stacked("Wv"), "wo": stacked("Wo"), "bo": stacked("bo").T,
        "nw": nw, "nwo": nwo, "norm_w": a["L2_xattn_norm_w"][:, None],
    }
    arrays = {f"in_{k}": _np.ascontiguousarray(v) for k, v in arrays.items()}
    nc = _bacc.Bacc("TRN2", target_bir_lowering=False, num_devices=1)
    args = [nc.dram_tensor(k, v.shape, _mybir.dt.from_np(v.dtype), kind="ExternalInput").ap()
            for k, v in arrays.items()]
    args.append(nc.dram_tensor("out_x", (B, T, C), _mybir.dt.float32, kind="ExternalOutput").ap())
    build_program(nc, *args)
    r = _run(nc, [arrays], core_ids=[0])
    return r.results[0]["out_x"]
```
